# Optimizing a Trainium2 kernel written in Bass

```python
import numpy as np
import jax
import jax.numpy as jnp

def _softmax(x, axis=-1):
    return jax.nn.softmax(x, axis=axis)

def _gelu(x):
    return jax.nn.gelu(x, approximate=True)

def _silu(x):
    return jax.nn.silu(x)

def _sigmoid(x):
    return jax.nn.sigmoid(x)

def _layernorm(x, axis=-1, eps=1e-05):
    m = jnp.mean(x, axis=axis, keepdims=True)
    v = jnp.var(x, axis=axis, keepdims=True)
    return (x - m) / jnp.sqrt(v + eps)

def _scatter_add(tgt, idx, src, axis=0):
    return tgt.at[idx].add(src)

def _segment_sum(src, seg, n):
    return jax.ops.segment_sum(src, seg, n)
kernel_name = 'mk_lm_tower_d1_tok_ids2048_r4_478724'

def setup_inputs(seed: int=0):
    np.random.seed(seed)
    _w = jnp.asarray

    def _rec_inputs():
        import jax
        import jax.numpy as jnp
        _rk = jax.random.key(seed)
        x = jax.random.randint(jax.random.fold_in(_rk, 1), (32, 512), 0, 12564, jnp.int32)
        return x
    x = _rec_inputs()

    def _L0_tok_setup():
        import jax, jax.numpy as jnp
        import numpy as np
        VOCAB = 50257
        EMBED_DIM = 512
        N_LAYERS = 2
        LOCAL_D = EMBED_DIM // 2 // N_LAYERS
        EMBD_D = EMBED_DIM - LOCAL_D * (2 * N_LAYERS - 1)
        KERNEL = 3
        B, T = (16, 512)

        def positional_encoding(max_len, d_model):
            depth = d_model // 2
            positions = jnp.arange(max_len, dtype=jnp.float32)[:, None]
            depths = jnp.arange(depth, dtype=jnp.float32)[None, :] / depth
            angle_rads = positions * (1.0 / 10000.0 ** depths)
            return jnp.concatenate([jnp.sin(angle_rads), jnp.cos(angle_rads)], axis=-1)

        def softpos_axis1(x, spos):
            n_subpos = spos.shape[0]
            m = x[:, :n_subpos, :]
            sel = jax.nn.softmax(m, axis=1)
            ext = jnp.einsum('bjt,jk->bkt', sel, spos)
            return jnp.concatenate([x, ext], axis=1)
        key = jax.random.key(seed)
        ks = jax.random.split(key, 6)
        return {'sequences': jax.random.randint(ks[0], (B, T), 0, VOCAB), 'emb_table': jax.random.normal(ks[1], (VOCAB, EMBD_D), dtype=jnp.float32), 'conv_w': jax.random.normal(ks[2], (LOCAL_D, EMBD_D, KERNEL), dtype=jnp.float32) * 0.05, 'conv_b': jax.random.normal(ks[3], (LOCAL_D,), dtype=jnp.float32) * 0.05, 'spos0': jax.random.normal(ks[4], (LOCAL_D, LOCAL_D), dtype=jnp.float32) * 0.05, 'spos1': jax.random.normal(ks[5], (LOCAL_D, LOCAL_D), dtype=jnp.float32) * 0.05}
    _L0_tok_all = _L0_tok_setup()
    _L0_tok_in = {k: v for k, v in _L0_tok_all.items() if k in ('emb_table', 'conv_w', 'conv_b', 'spos0', 'spos1')}
    del _L0_tok_all

    def _L0_attn_setup():
        import jax, jax.numpy as jnp
        import numpy as np
        B, S, H = (4, 512, 512)
        key = jax.random.key(seed)
        k1, k2, k3 = jax.random.split(key, 3)
        xav_qkv = float(np.sqrt(6.0 / (H + 3 * H)))
        xav_out = float(np.sqrt(6.0 / (H + H)))
        return {'hidden_states': jax.random.normal(k1, (B, S, H), dtype=jnp.float32), 'w_qkv': jax.random.uniform(k2, (3 * H, H), minval=-xav_qkv, maxval=xav_qkv, dtype=jnp.float32), 'b_qkv': jnp.zeros((3 * H,), dtype=jnp.float32), 'w_out': jax.random.uniform(k3, (H, H), minval=-xav_out, maxval=xav_out, dtype=jnp.float32), 'b_out': jnp.zeros((H,), dtype=jnp.float32)}
    _L0_attn_all = _L0_attn_setup()
    _L0_attn_in = {k: v for k, v in _L0_attn_all.items() if k in ('w_qkv', 'b_qkv', 'w_out', 'b_out')}
    del _L0_attn_all

    def _L0_ffn_setup():
        import jax, jax.numpy as jnp
        import numpy as np
        B, S, D_IN, D_OUT = (4, 512, 512, 512)
        EPS = 1e-10
        key = jax.random.key(seed)
        kx, kw, kb = jax.random.split(key, 3)
        x = jax.random.normal(kx, (B, S, D_IN), dtype=jnp.float32)
        weight = jax.random.normal(kw, (D_OUT, D_IN), dtype=jnp.float32) * 0.02
        bias = jax.random.normal(kb, (D_OUT,), dtype=jnp.float32) * 0.02
        return {'x': x, 'weight': weight, 'bias': bias}
    _L0_ffn_all = _L0_ffn_setup()
    _L0_ffn_in = {k: v for k, v in _L0_ffn_all.items() if k in ('weight', 'bias')}
    del _L0_ffn_all
    return {'x': x, 'L0_tok_emb_table': _L0_tok_in['emb_table'], 'L0_tok_conv_w': _L0_tok_in['conv_w'], 'L0_tok_conv_b': _L0_tok_in['conv_b'], 'L0_tok_spos0': _L0_tok_in['spos0'], 'L0_tok_spos1': _L0_tok_in['spos1'], 'L0_attn_w_qkv': _L0_attn_in['w_qkv'], 'L0_attn_b_qkv': _L0_attn_in['b_qkv'], 'L0_attn_w_out': _L0_attn_in['w_out'], 'L0_attn_b_out': _L0_attn_in['b_out'], 'L0_ffn_weight': _L0_ffn_in['weight'], 'L0_ffn_bias': _L0_ffn_in['bias']}

def reference(x, L0_tok_emb_table, L0_tok_conv_w, L0_tok_conv_b, L0_tok_spos0, L0_tok_spos1, L0_attn_w_qkv, L0_attn_b_qkv, L0_attn_w_out, L0_attn_b_out, L0_ffn_weight, L0_ffn_bias):
    import jax
    import jax.numpy as jnp

    def _L0_tok_ref(sequences, emb_table, conv_w, conv_b, spos0, spos1):
        import jax, jax.numpy as jnp
        import numpy as np
        VOCAB = 50257
        EMBED_DIM = 512
        N_LAYERS = 2
        LOCAL_D = EMBED_DIM // 2 // N_LAYERS
        EMBD_D = EMBED_DIM - LOCAL_D * (2 * N_LAYERS - 1)
        KERNEL = 3
        B, T = (16, 512)

        def positional_encoding(max_len, d_model):
            depth = d_model // 2
            positions = jnp.arange(max_len, dtype=jnp.float32)[:, None]
            depths = jnp.arange(depth, dtype=jnp.float32)[None, :] / depth
            angle_rads = positions * (1.0 / 10000.0 ** depths)
            return jnp.concatenate([jnp.sin(angle_rads), jnp.cos(angle_rads)], axis=-1)

        def softpos_axis1(x, spos):
            n_subpos = spos.shape[0]
            m = x[:, :n_subpos, :]
            sel = jax.nn.softmax(m, axis=1)
            ext = jnp.einsum('bjt,jk->bkt', sel, spos)
            return jnp.concatenate([x, ext], axis=1)
        seq_len = sequences.shape[1]
        x = emb_table[sequences] * jnp.sqrt(jnp.float32(EMBD_D))
        x = x + positional_encoding(seq_len, EMBD_D)[None]
        x = jnp.transpose(x, (0, 2, 1))
        dilation = 1
        x_pad = jnp.pad(x, ((0, 0), (0, 0), ((KERNEL - 1) * dilation, 0)))
        xc = jax.lax.conv_general_dilated(x_pad, conv_w, window_strides=(1,), padding='VALID', rhs_dilation=(dilation,), dimension_numbers=('NCH', 'OIH', 'NCH'))
        xc = xc + conv_b[None, :, None]
        y0 = softpos_axis1(x, spos0)
        y1 = softpos_axis1(xc, spos1)
        return jnp.concatenate([y0, y1], axis=1)

    def _L0_attn_ref(hidden_states, w_qkv, b_qkv, w_out, b_out):
        import jax, jax.numpy as jnp
        import numpy as np
        B, S, H = (4, 512, 512)
        Bc, Sc, Hc = hidden_states.shape
        scaling = jnp.sqrt(jnp.asarray(Hc, hidden_states.dtype))
        qkv = jnp.einsum('bsh,oh->bso', hidden_states, w_qkv) + b_qkv
        q, k, v = jnp.split(qkv, 3, axis=-1)
        scores = jnp.einsum('bqh,bkh->bqk', q, k) / scaling
        probs = jax.nn.softmax(scores, axis=-1)
        context = jnp.einsum('bqk,bkh->bqh', probs, v)
        out = jnp.einsum('bsh,oh->bso', context, w_out) + b_out
        return out

    def _L0_ffn_ref(x, weight, bias):
        import jax, jax.numpy as jnp
        import numpy as np
        B, S, D_IN, D_OUT = (4, 512, 512, 512)
        EPS = 1e-10
        scale = jnp.mean(jnp.abs(weight))
        w_t = jnp.clip(jnp.round(weight / (scale + EPS)), -1.0, 1.0)
        w_ste = weight + jax.lax.stop_gradient(w_t * scale - weight)
        return jnp.einsum('bsi,oi->bso', x, w_ste) + bias
    h = _L0_tok_ref(x, L0_tok_emb_table, L0_tok_conv_w, L0_tok_conv_b, L0_tok_spos0, L0_tok_spos1)
    h = h + _L0_attn_ref(_layernorm(h, axis=-1), L0_attn_w_qkv, L0_attn_b_qkv, L0_attn_w_out, L0_attn_b_out)
    h = h + _L0_ffn_ref(_layernorm(h, axis=-1), L0_ffn_weight, L0_ffn_bias)
    return h

_drawn_inputs = setup_inputs


def setup_inputs(seed=0):
    import zlib

    import numpy as np

    out = dict(_drawn_inputs(seed))
    spreads = {'L0_attn_b_qkv': (0.0, 0.374), 'L0_attn_b_out': (0.0, 0.371)}
    factors = {'L0_tok_conv_b': 8.0,
     'L0_tok_spos0': 6.897,
     'L0_tok_spos1': 7.036,
     'L0_attn_w_qkv': 6.316,
     'L0_ffn_bias': 25.491}
    for name, (base, spread) in spreads.items():
        noise = np.random.default_rng([zlib.crc32(name.encode()), seed]).standard_normal(out[name].shape)
        drawn = base * np.exp(spread * noise) if base else spread * noise
        out[name] = jnp.asarray(drawn.astype(out[name].dtype))
    for name, factor in factors.items():
        out[name] = (out[name] * factor).astype(out[name].dtype)
    return out
```

```python
from contextlib import ExitStack

import concourse.bass as bass
from concourse import mybir

ALU = mybir.AluOpType
ACT = mybir.ActivationFunctionType
F32 = mybir.dt.float32
F16 = mybir.dt.float16
I32 = mybir.dt.int32
AX_X = mybir.AxisListType.X

P = 128
T = 512
NT = T // P
PAD = 2
TAPS = 3
LN_EPS = 1e-5
W_EPS = 1e-10
SCALE = float(T) ** -0.5

X_BLK, XEXT_BLK, CONV_BLK, CEXT_BLK = range(4)

SOFTPOS_STEPS = 5
LN1_STEPS = 10
LN2_STEPS = 4


def lm_tower(nc, ids, emb, pos, conv_w, conv_b, spos0, spos1, w_qkv, b_qkv, w_out_t, b_out, w_ffn_t, b_ffn, out):
    B = out.shape[0]
    ctx = ExitStack()
    with ctx:
        def sb(name, shape, dt=F32):
            return ctx.enter_context(nc.sbuf_tensor(name, shape, dt))

        def sem(name):
            return ctx.enter_context(nc.semaphore(name))

        ids_sb = sb("ids_sb", [P, B * NT], I32)
        ident = sb("ident", [P, P])
        ones = sb("ones", [P, P])
        pos_sb = sb("pos_sb", [P, NT, P])
        conv_w_sb = sb("conv_w_sb", [P, TAPS, P])
        conv_b_sb = sb("conv_b_sb", [P, 1])
        spos_sb = sb("spos_sb", [P, 2, P])
        w_qkv_sb = sb("w_qkv_sb", [P, 3 * NT, T])
        b_qkv_sb = sb("b_qkv_sb", [P, 3 * NT])
        w_out_sb = sb("w_out_sb", [P, NT, T])
        w_ffn_sb = sb("w_ffn_sb", [P, NT, T])
        b_out_sb = sb("b_out_sb", [P, T])
        b_ffn_sb = sb("b_ffn_sb", [P, T])
        b_wide = sb("b_wide", [P, 2, NT, P])
        m_hi = sb("m_hi", [P, NT, T], F16)
        m_lo = sb("m_lo", [P, NT, T], F16)
        vo_hi = sb("vo_hi", [P, NT, T], F16)
        vo_lo = sb("vo_lo", [P, NT, T], F16)
        tern = sb("tern", [P, NT, T], F16)
        below = sb("below", [P, NT, T])
        q_bias = sb("q_bias", [P, NT])
        key_row = sb("key_row", [P, T])
        bqbk = sb("bqbk", [P, 1])
        attn_bias = sb("attn_bias", [P, T])
        wsum = sb("wsum", [P, 1])
        wscale = sb("wscale", [P, 3])

        idx = sb("idx", [P, NT], I32)
        gathered_sb = sb("gathered_sb", [P, NT, P])
        xe = sb("xe", [P, NT, P])
        ch_max = sb("ch_max", [P, 2, NT])
        ch_sum = sb("ch_sum", [P, 2, NT])
        ch_rcp = sb("ch_rcp", [P, 2, NT])
        shifted = sb("shifted", [P, NT, P])
        ch_exp = sb("ch_exp", [P, NT, P])
        sel = sb("sel", [P, NT, P])
        sel_t = sb("sel_t", [P, T])
        h = sb("h", [P, NT, PAD + T])
        h_attn = sb("h_attn", [P, NT, T])
        stats1 = sb("stats1", [P, NT, 6])
        mv1 = sb("mv1", [P, NT, 2])
        rstd1 = sb("rstd1", [P, 4, NT])
        n = sb("n", [P, NT, T])
        junk = sb("junk", [P, T])
        row_term = sb("row_term", [P, NT])
        nt_hi = sb("nt_hi", [P, NT, T], F16)
        nt_lo = sb("nt_lo", [P, NT, T], F16)
        q_hi = sb("q_hi", [P, NT, T], F16)
        q_lo = sb("q_lo", [P, NT, T], F16)
        v_hi = sb("v_hi", [P, NT, T], F16)
        v_lo = sb("v_lo", [P, NT, T], F16)
        s_max = sb("s_max", [P, NT])
        s_top = sb("s_top", [P, NT])
        s_bias = sb("s_bias", [P, NT])
        prob = sb("prob", [P, NT, T])
        p_sum = sb("p_sum", [P, NT])
        p_rcp = sb("p_rcp", [P, NT])
        pt_hi = sb("pt_hi", [P, NT, NT, P], F16)
        pt_lo = sb("pt_lo", [P, NT, NT, P], F16)
        h1 = sb("h1", [P, NT, T])
        h1_ffn = sb("h1_ffn", [P, NT, T])
        stats2 = sb("stats2", [P, NT, 6])
        mv2 = sb("mv2", [P, NT, 2])
        rstd2 = sb("rstd2", [P, 4, NT])
        n2 = sb("n2", [P, NT, T])
        n2t_hi = sb("n2t_hi", [P, NT, NT, P], F16)
        n2t_lo = sb("n2t_lo", [P, NT, NT, P], F16)
        y = sb("y", [P, NT, T])
        ln_eps = sb("ln_eps", [P, 1])
        spare = sb("spare", [P, 1])

        mm = [ctx.enter_context(nc.psum_tensor(f"mm{k}", [P, T], F32)) for k in range(4)]
        tp = [ctx.enter_context(nc.psum_tensor(f"tp{k}", [P, T], F32)) for k in range(2)]
        fr = [ctx.enter_context(nc.psum_tensor(f"fr{k}", [P, T], F32)) for k in range(2)]

        ids_loaded = sem("ids_loaded")
        tower_loaded = sem("tower_loaded")
        attn_loaded = sem("attn_loaded")
        out_loaded = sem("out_loaded")
        ffn_loaded = sem("ffn_loaded")
        ident_zeroed = sem("ident_zeroed")
        consts_ready = sem("consts_ready")
        pads_zeroed = sem("pads_zeroed")
        wide_ready = sem("wide_ready")
        merged_ready = sem("merged_ready")
        merged_hi = sem("merged_hi")
        merged_split = sem("merged_split")
        bias_mm_ready = sem("bias_mm_ready")
        bias_ready = sem("bias_ready")
        abs_ready = sem("abs_ready")
        abs_total = sem("abs_total")
        tern_step = sem("tern_step")
        tern_ready = sem("tern_ready")
        idx_ready = sem("idx_ready")
        rows_gathered = sem("rows_gathered")
        xe_ready = sem("xe_ready")
        x_t_ready = sem("x_t_ready")
        h_x_ready = sem("h_x_ready")
        softpos_step = sem("softpos_step")
        ch_exp_ready = sem("ch_exp_ready")
        sel_t_ready = sem("sel_t_ready")
        sel_t_copied = sem("sel_t_copied")
        conv_ready = sem("conv_ready")
        h_conv_ready = sem("h_conv_ready")
        conv_t_ready = sem("conv_t_ready")
        ext_ready = sem("ext_ready")
        h_ext_ready = sem("h_ext_ready")
        ln1_step = sem("ln1_step")
        ln1_root = sem("ln1_root")
        n_scale_ready = sem("n_scale_ready")
        n_ready = sem("n_ready")
        row_term_ready = sem("row_term_ready")
        h_attn_ready = sem("h_attn_ready")
        nt_ready, nt_high, nt_split = sem("nt_ready"), sem("nt_high"), sem("nt_split")
        q_ready, q_high, q_split = sem("q_ready"), sem("q_high"), sem("q_split")
        v_ready, v_high, v_split = sem("v_ready"), sem("v_high"), sem("v_split")
        scores_ready = sem("scores_ready")
        shift_step = sem("shift_step")
        prob_ready = sem("prob_ready")
        pt_ready, pt_high, pt_split = sem("pt_ready"), sem("pt_high"), sem("pt_split")
        p_rcp_ready = sem("p_rcp_ready")
        o_ready = sem("o_ready")
        h1_ready = sem("h1_ready")
        h1_ffn_ready = sem("h1_ffn_ready")
        ln2_step = sem("ln2_step")
        ln2_root = sem("ln2_root")
        n2_scale_ready = sem("n2_scale_ready")
        n2_ready = sem("n2_ready")
        n2t_ready, n2t_high, n2t_split = sem("n2t_ready"), sem("n2t_high"), sem("n2t_split")
        f_ready = sem("f_ready")
        y_ready = sem("y_ready")
        y_stored = sem("y_stored")

        def half(j):
            return slice(j * P, (j + 1) * P)

        block = ctx.enter_context(nc.Block())

        @block.sync
        def _(sp):
            sp.sem_inc(y_stored, 64)
            sp.dma_start(ids_sb[:, :], ids).then_inc(ids_loaded, 16)
            sp.dma_start(pos_sb[:, :, :], pos).then_inc(tower_loaded, 16)
            sp.dma_start(conv_w_sb[:, :, :], conv_w).then_inc(tower_loaded, 16)
            sp.dma_start(conv_b_sb[:, :], conv_b).then_inc(tower_loaded, 16)
            sp.dma_start(spos_sb[:, 0, :], spos0).then_inc(tower_loaded, 16)
            sp.dma_start(spos_sb[:, 1, :], spos1).then_inc(tower_loaded, 16)
            for part in range(2):
                sp.dma_start(w_qkv_sb[:, part * NT:(part + 1) * NT, :],
                             w_qkv[part * T:(part + 1) * T, :].rearrange("(c p) t -> p c t", p=P)
                             ).then_inc(attn_loaded, 16)
            sp.dma_start(b_qkv_sb[:, :], b_qkv).then_inc(attn_loaded, 16)
            sp.dma_start(w_qkv_sb[:, 2 * NT:, :],
                         w_qkv[2 * T:, :].rearrange("(c p) t -> p c t", p=P)).then_inc(out_loaded, 16)
            sp.dma_start(w_out_sb[:, :, :], w_out_t.rearrange("(c p) t -> p c t", p=P)).then_inc(out_loaded, 16)
            sp.dma_start(b_out_sb[:, :], b_out.partition_broadcast(P)).then_inc(out_loaded, 16)
            sp.dma_start(w_ffn_sb[:, :, :], w_ffn_t.rearrange("(c p) t -> p c t", p=P)).then_inc(ffn_loaded, 16)
            sp.dma_start(b_ffn_sb[:, :], b_ffn.partition_broadcast(P)).then_inc(ffn_loaded, 16)

            with sp.Fori(0, B) as b:
                for j in range(NT):
                    sp.wait_ge(y_ready, 4 * b + (j + 5))
                    sp.dma_start(out[b, half(j), :], y[:, j, :]).then_inc(y_stored, 16)
            sp.wait_ge(y_stored, 64 * (B + 1))

        @block.gpsimd
        def _(pool):
            nc.gpsimd.memset(ident[:, :], 0.0).then_inc(ident_zeroed, 1)
            nc.gpsimd.memset(h[:, :, 0:PAD], 0.0).then_inc(pads_zeroed, 1)
            nc.gpsimd.memset(ones[:, :], 1.0).then_inc(consts_ready, 1)
            nc.gpsimd.memset(ln_eps[:, :], LN_EPS).then_inc(consts_ready, 1)
            pool.wait_ge(ident_zeroed, 1)
            nc.gpsimd.affine_select(out=ident[:, :], in_=ident[:, :], compare_op=ALU.not_equal, fill=1.0,
                                    base=0, pattern=[[-1, P]], channel_multiplier=1).then_inc(consts_ready, 1)
            pool.wait_ge(ids_loaded, 16)

            def take_ids(b):
                nc.gpsimd.tensor_copy(idx[:, :], ids_sb[:, bass.ts(b, NT)]).then_inc(idx_ready, 1)

            def gather():
                for c in range(NT):
                    nc.gpsimd.indirect_dma_start(
                        out=gathered_sb[:, c, :], out_offset=None, in_=emb,
                        in_offset=bass.IndirectOffsetOnAxis(ap=idx[:, c:c + 1], axis=0)
                    ).then_inc(rows_gathered, 16)

            def add_attention_bias(j):
                nc.gpsimd.tensor_tensor(out=h_attn[:, j, :], in0=h[:, j, PAD:], in1=attn_bias[:, :],
                                        op=ALU.add).then_inc(h_attn_ready, 1)

            def add_ffn_bias(b):
                pool.wait_ge(y_ready, 4 * b + 4)
                for j in range(NT):
                    pool.wait_ge(h1_ready, 4 * b + (j + 1))
                    nc.gpsimd.tensor_tensor(out=h1_ffn[:, j, :], in0=h1[:, j, :], in1=b_ffn_sb[:, :],
                                            op=ALU.add).then_inc(h1_ffn_ready, 1)

            take_ids(0)
            pool.wait_ge(idx_ready, 1)
            gather()
            pool.wait_ge(xe_ready, 1)
            pool.wait_ge(rows_gathered, 64)
            take_ids(1)
            pool.wait_ge(idx_ready, 2)
            gather()
            pool.wait_ge(bias_ready, 4)
            pool.wait_ge(ffn_loaded, 32)

            def batch(b, more):
                pool.wait_ge(n_ready, 4 * b + 4)
                for j in range(NT - 1):
                    add_attention_bias(j)
                if more:
                    pool.wait_ge(xe_ready, b + 2)
                    take_ids(b + 2)
                    pool.wait_ge(idx_ready, b + 3)
                add_attention_bias(NT - 1)
                if more:
                    gather()
                add_ffn_bias(b)

            with pool.Fori(0, B - 2) as b:
                batch(b, True)
            batch(B - 2, False)
            batch(B - 1, False)

        @block.tensor
        def _(pe):
            def transpose4(dst, src, done):
                for c in range(NT):
                    last = nc.tensor.transpose(dst[:, half(c)], src(c), ident[:, :])
                last.then_inc(done, 1)

            def split_product(dst, a_hi, a_lo, b_hi, b_lo, done):
                for c in range(NT):
                    nc.tensor.matmul(dst[:, :], a_hi(c), b_hi(c), start=(c == 0), stop=False)
                    nc.tensor.matmul(dst[:, :], a_hi(c), b_lo(c), start=False, stop=False)
                    last = nc.tensor.matmul(dst[:, :], a_lo(c), b_hi(c), start=False, stop=(c == NT - 1))
                last.then_inc(done, 1)

            def x_transpose(f):
                pe.wait_ge(xe_ready, f + 1)
                pe.wait_ge(h_ext_ready, 2 * f)
                transpose4(fr[0], lambda c: xe[:, c, :], x_t_ready)

            def sel_transpose(f, w):
                pe.wait_ge(softpos_step, SOFTPOS_STEPS * (2 * f + (w + 1)))
                if w == 0:
                    pe.wait_ge(sel_t_copied, 2 * f)
                transpose4(fr[1], lambda c: sel[:, c, :], sel_t_ready)

            def convolution(f):
                pe.wait_ge(h_x_ready, f + 1)
                for k in range(TAPS):
                    last = nc.tensor.matmul(fr[0][:, :], conv_w_sb[:, k, :], h[:, X_BLK, k:k + T],
                                            start=(k == 0), stop=(k == TAPS - 1))
                last.then_inc(conv_ready, 1)

            def conv_transpose(f):
                pe.wait_ge(h_conv_ready, f + 1)
                pe.wait_ge(sel_t_copied, 2 * f + 1)
                transpose4(fr[1], lambda c: h[:, CONV_BLK, PAD + c * P:PAD + (c + 1) * P], conv_t_ready)

            def extension(f, w):
                pe.wait_ge(sel_t_copied, 2 * f + (w + 1))
                if w == 0:
                    pe.wait_ge(h_conv_ready, f + 1)
                else:
                    pe.wait_ge(h_ext_ready, 2 * f + 1)
                nc.tensor.matmul(fr[0][:, :], spos_sb[:, w, :], sel_t[:, :], start=True, stop=True
                                 ).then_inc(ext_ready, 1)

            def nt_transpose(f, j, bank):
                pe.wait_ge(n_ready, 4 * f + 4)
                transpose4(fr[bank], lambda c: n[:, c, half(j)], nt_ready)

            def queries(b, j, bank):
                pe.wait_ge(nt_split, 4 * b + 4)
                split_product(mm[bank], lambda c: m_hi[:, c, half(j)], lambda c: m_lo[:, c, half(j)],
                              lambda c: nt_hi[:, c, :], lambda c: nt_lo[:, c, :], q_ready)

            def values(b, j):
                if j >= 2:
                    pe.wait_ge(y_ready, 4 * b + 4)
                split_product(mm[j], lambda c: nt_hi[:, c, half(j)], lambda c: nt_lo[:, c, half(j)],
                              lambda c: vo_hi[:, c, :], lambda c: vo_lo[:, c, :], v_ready)

            def scores(b, j):
                pe.wait_ge(v_split, 4 * b + (j + 1))
                pe.wait_ge(q_split, 4 * b + 4)
                split_product(mm[j], lambda c: q_hi[:, c, half(j)], lambda c: q_lo[:, c, half(j)],
                              lambda c: nt_hi[:, c, :], lambda c: nt_lo[:, c, :], scores_ready)

            def prob_transpose(b, j, bank):
                pe.wait_ge(prob_ready, 4 * b + (j + 1))
                transpose4(tp[bank], lambda c: prob[:, j, half(c)], pt_ready)

            def attend(b, j):
                pe.wait_ge(pt_split, 4 * b + (j + 1))
                split_product(mm[j], lambda c: pt_hi[:, j, c, :], lambda c: pt_lo[:, j, c, :],
                              lambda c: v_hi[:, c, :], lambda c: v_lo[:, c, :], o_ready)

            def n2_transpose(b, j, bank):
                pe.wait_ge(n2_ready, 4 * b + (j + 1))
                transpose4(tp[bank], lambda c: n2[:, j, half(c)], n2t_ready)

            def ffn(b, j, bank):
                pe.wait_ge(n2t_split, 4 * b + (j + 1))
                for c in range(NT):
                    nc.tensor.matmul(mm[bank][:, :], n2t_hi[:, j, c, :], tern[:, c, :],
                                     start=(c == 0), stop=False)
                    last = nc.tensor.matmul(mm[bank][:, :], n2t_lo[:, j, c, :], tern[:, c, :],
                                            start=False, stop=(c == NT - 1))
                last.then_inc(f_ready, 1)

            pe.wait_ge(consts_ready, 3)
            pe.wait_ge(pads_zeroed, 1)
            x_transpose(0)
            pe.wait_ge(tower_loaded, 80)
            sel_transpose(0, 0)
            convolution(0)
            extension(0, 0)
            conv_transpose(0)
            sel_transpose(0, 1)
            extension(0, 1)

            pe.wait_ge(attn_loaded, 48)
            for j in range(NT):
                for c in range(NT):
                    last = nc.tensor.matmul(mm[j][:, :], w_qkv_sb[:, c, half(j)], w_qkv_sb[:, NT + c, :],
                                            start=(c == 0), stop=(c == NT - 1))
                last.then_inc(merged_ready, 1)
            pe.wait_ge(wide_ready, 8)
            for j in range(NT):
                for c in range(NT):
                    nc.tensor.matmul(tp[0][:, j:j + 1], w_qkv_sb[:, NT + c, half(j)], b_qkv_sb[:, c:c + 1],
                                     start=(c == 0), stop=(c == NT - 1))
            for c in range(NT):
                last = nc.tensor.matmul(tp[0][:, NT:NT + 1], b_wide[:, 0, c, :], b_qkv_sb[:, c:c + 1],
                                        start=(c == 0), stop=(c == NT - 1))
            last.then_inc(bias_mm_ready, 1)
            for c in range(NT):
                last = nc.tensor.matmul(tp[1][:, :], b_wide[:, 0, c, :], w_qkv_sb[:, c, :],
                                        start=(c == 0), stop=(c == NT - 1))
            last.then_inc(bias_mm_ready, 1)
            pe.wait_ge(out_loaded, 48)
            for j in range(NT):
                pe.wait_ge(merged_split, j + 1)
                for c in range(NT):
                    last = nc.tensor.matmul(mm[j][:, :], w_qkv_sb[:, 2 * NT + c, half(j)], w_out_sb[:, c, :],
                                            start=(c == 0), stop=(c == NT - 1))
                last.then_inc(merged_ready, 1)
            pe.wait_ge(h_ext_ready, 2)
            for c in range(NT):
                last = nc.tensor.matmul(fr[0][:, :], b_wide[:, 1, c, :], w_out_sb[:, c, :],
                                        start=(c == 0), stop=(c == NT - 1))
            last.then_inc(bias_mm_ready, 1)
            pe.wait_ge(abs_ready, 1)
            pe.wait_ge(sel_t_copied, 2)
            nc.tensor.matmul(fr[1][:, 0:1], ones[:, :], wsum[:, :], start=True, stop=True).then_inc(abs_total, 1)
            pe.wait_ge(bias_ready, 4)
            nt_transpose(0, 0, 0)
            pe.wait_ge(tern_step, 1)
            nt_transpose(0, 1, 1)
            pe.wait_ge(nt_split, 2)
            nt_transpose(0, 2, 0)
            nt_transpose(0, 3, 1)
            for j in range(NT):
                pe.wait_ge(merged_split, NT + j + 1)
                queries(0, j, j)
            pe.wait_ge(tern_ready, 1)
            pe.wait_ge(q_split, 4)

            def batch(b, tower):
                f = b + 1
                values(b, 0)
                if tower:
                    x_transpose(f)
                    sel_transpose(f, 0)
                values(b, 1)
                if tower:
                    convolution(f)
                values(b, 2)
                if tower:
                    extension(f, 0)
                    conv_transpose(f)
                values(b, 3)
                scores(b, 0)
                if tower:
                    sel_transpose(f, 1)
                scores(b, 1)
                if tower:
                    extension(f, 1)
                scores(b, 2)
                prob_transpose(b, 0, 0)
                scores(b, 3)
                prob_transpose(b, 1, 1)
                attend(b, 0)
                prob_transpose(b, 2, 0)
                attend(b, 1)
                prob_transpose(b, 3, 1)
                if tower:
                    pe.wait_ge(h_ext_ready, 2 * f + 2)
                    nt_transpose(f, 0, 0)
                    nt_transpose(f, 1, 1)
                attend(b, 2)
                if tower:
                    pe.wait_ge(nt_split, 4 * f + 2)
                    nt_transpose(f, 2, 0)
                    nt_transpose(f, 3, 1)
                attend(b, 3)
                if tower:
                    pe.wait_ge(h1_ready, 4 * b + 1)
                    queries(f, 0, 0)
                n2_transpose(b, 0, 0)
                if tower:
                    pe.wait_ge(h1_ready, 4 * b + 2)
                    queries(f, 1, 1)
                n2_transpose(b, 1, 1)
                pe.wait_ge(h1_ready, 4 * b + 3)
                ffn(b, 0, 2)
                if tower:
                    pe.wait_ge(h1_ready, 4 * b + 4)
                    queries(f, 2, 3)
                n2_transpose(b, 2, 0)
                if tower:
                    pe.wait_ge(q_split, 4 * f + 1)
                ffn(b, 1, 0)
                if tower:
                    pe.wait_ge(q_split, 4 * f + 2)
                    queries(f, 3, 1)
                n2_transpose(b, 3, 1)
                pe.wait_ge(y_ready, 4 * b + 5)
                ffn(b, 2, 2)
                if tower:
                    pe.wait_ge(q_split, 4 * f + 3)
                ffn(b, 3, 3)
                pe.wait_ge(y_ready, 4 * b + 6)
                if tower:
                    pe.wait_ge(q_split, 4 * f + 4)

            with pe.Fori(0, B - 1) as b:
                batch(b, True)
            batch(B - 1, False)

        @block.scalar
        def _(act):
            def high(dst, src, ready, ready_at, done, bias=None):
                act.wait_ge(ready, ready_at)
                if bias is None:
                    nc.scalar.activation(dst, src, ACT.Copy).then_inc(done, 1)
                else:
                    nc.scalar.activation(dst, src, ACT.Identity, bias=bias).then_inc(done, 1)

            def channel_exp(f, w):
                act.wait_ge(softpos_step, SOFTPOS_STEPS * (2 * f + w) + 2)
                nc.scalar.activation(ch_exp[:, :, :], shifted[:, :, :], ACT.Exp).then_inc(ch_exp_ready, 1)

            def store_x(f):
                act.wait_ge(x_t_ready, f + 1)
                act.wait_ge(h_attn_ready, 4 * f)
                nc.scalar.activation(h[:, X_BLK, PAD:], fr[0][:, :], ACT.Copy).then_inc(h_x_ready, 1)

            def store_sel(f, w):
                act.wait_ge(sel_t_ready, 2 * f + (w + 1))
                nc.scalar.activation(sel_t[:, :], fr[1][:, :], ACT.Copy).then_inc(sel_t_copied, 1)

            def store_conv(f):
                act.wait_ge(conv_ready, f + 1)
                nc.scalar.activation(h[:, CONV_BLK, PAD:], fr[0][:, :], ACT.Identity, bias=conv_b_sb[:, :]
                                     ).then_inc(h_conv_ready, 1)

            def store_ext(f, w):
                act.wait_ge(ext_ready, 2 * f + (w + 1))
                blk = XEXT_BLK if w == 0 else CEXT_BLK
                nc.scalar.activation(h[:, blk, PAD:], fr[0][:, :], ACT.Copy).then_inc(h_ext_ready, 1)

            def rsqrt_guess(out_ln, out_rs, var, ready, ready_at, done, done_at):
                act.wait_ge(ready, ready_at)
                nc.scalar.activation(out_ln, var, ACT.Ln, bias=ln_eps[:, :]).then_inc(done, 1)
                act.wait_ge(done, done_at)
                nc.scalar.activation(out_rs, out_ln, ACT.Exp, scale=-0.5).then_inc(done, 1)

            def ln1_guess(f):
                rsqrt_guess(rstd1[:, 0, :], rstd1[:, 1, :], mv1[:, :, 1], ln1_step, LN1_STEPS * f + 8,
                            ln1_root, 2 * f + 1)

            def ln2_guess(b, j):
                rsqrt_guess(rstd2[:, 0, j:j + 1], rstd2[:, 1, j:j + 1], mv2[:, j, 1:2],
                            ln2_step, LN2_STEPS * (4 * b + j) + 2, ln2_root, 2 * (4 * b + j) + 1)

            def nt_half(f, j, bank):
                high(nt_hi[:, j, :], fr[bank][:, :], nt_ready, 4 * f + (j + 1), nt_high)

            def query_half(b, j, bank):
                high(q_hi[:, j, :], mm[bank][:, :], q_ready, 4 * b + (j + 1), q_high, bias=q_bias[:, j:j + 1])

            def value_half(b, j):
                high(v_hi[:, j, :], mm[j][:, :], v_ready, 4 * b + (j + 1), v_high)

            def score_exp(b, j):
                act.wait_ge(shift_step, 3 * (4 * b + j) + 3)
                nc.scalar.activation(prob[:, j, :], mm[j][:, :], ACT.Exp, bias=s_bias[:, j:j + 1], scale=SCALE,
                                     accum_out=p_sum[:, j:j + 1]).then_inc(prob_ready, 1)

            def prob_half(b, j, bank):
                high(pt_hi[:, j, :, :].rearrange("p c k -> p (c k)"), tp[bank][:, :],
                     pt_ready, 4 * b + (j + 1), pt_high)

            def n2_half(b, j, bank):
                high(n2t_hi[:, j, :, :].rearrange("p c k -> p (c k)"), tp[bank][:, :],
                     n2t_ready, 4 * b + (j + 1), n2t_high)

            act.wait_ge(consts_ready, 3)
            nc.scalar.preload_act_table_set("natural_log_exp_and_others")
            channel_exp(0, 0)
            store_x(0)
            act.wait_ge(tower_loaded, 80)
            store_sel(0, 0)
            store_conv(0)
            store_ext(0, 0)
            channel_exp(0, 1)
            store_sel(0, 1)
            store_ext(0, 1)
            ln1_guess(0)
            for j in range(NT):
                high(m_hi[:, j, :], mm[j][:, :], merged_ready, j + 1, merged_hi)
            for j in range(NT):
                high(vo_hi[:, j, :], mm[j][:, :], merged_ready, NT + j + 1, merged_hi)
            for j, bank in enumerate((0, 1, 0, 1)):
                nt_half(0, j, bank)
            act.wait_ge(bias_ready, 2)
            for j in range(NT):
                query_half(0, j, j)
            channel_exp(1, 0)

            def batch(b, tower, embed_next):
                f = b + 1
                value_half(b, 0)
                if tower:
                    store_x(f)
                    store_sel(f, 0)
                value_half(b, 1)
                if tower:
                    store_conv(f)
                value_half(b, 2)
                if tower:
                    store_ext(f, 0)
                    channel_exp(f, 1)
                value_half(b, 3)
                score_exp(b, 0)
                if tower:
                    store_sel(f, 1)
                score_exp(b, 1)
                if tower:
                    store_ext(f, 1)
                    ln1_guess(f)
                score_exp(b, 2)
                prob_half(b, 0, 0)
                prob_half(b, 1, 1)
                score_exp(b, 3)
                prob_half(b, 2, 0)
                ln2_guess(b, 0)
                prob_half(b, 3, 1)
                if tower:
                    nt_half(f, 0, 0)
                    nt_half(f, 1, 1)
                ln2_guess(b, 1)
                if tower:
                    nt_half(f, 2, 0)
                    nt_half(f, 3, 1)
                ln2_guess(b, 2)
                ln2_guess(b, 3)
                if tower:
                    query_half(f, 0, 0)
                n2_half(b, 0, 0)
                if tower:
                    query_half(f, 1, 1)
                n2_half(b, 1, 1)
                if tower:
                    query_half(f, 2, 3)
                n2_half(b, 2, 0)
                if tower:
                    query_half(f, 3, 1)
                n2_half(b, 3, 1)
                if embed_next:
                    channel_exp(f + 1, 0)

            with act.Fori(0, B - 2) as b:
                batch(b, True, True)
            batch(B - 2, True, False)
            batch(B - 1, False, False)

        @block.vector
        def _(dve):
            def low(dst, src, hi, high_done, at, done, bias=None):
                dve.wait_ge(high_done, at)
                if bias is None:
                    nc.vector.tensor_tensor(out=dst, in0=src, in1=hi, op=ALU.subtract).then_inc(done, 1)
                else:
                    nc.vector.scalar_tensor_tensor(out=dst, in0=src, scalar=bias, in1=hi, op0=ALU.add,
                                                   op1=ALU.subtract).then_inc(done, 1)

            def embed(f):
                dve.wait_ge(rows_gathered, 64 * (f + 1))
                if isinstance(f, int):
                    dve.wait_ge(tower_loaded, 80)
                nc.vector.scalar_tensor_tensor(out=xe[:, :, :], in0=gathered_sb[:, :, :], scalar=float(P) ** 0.5,
                                               in1=pos_sb[:, :, :], op0=ALU.mult, op1=ALU.add).then_inc(xe_ready, 1)

            def channel_shift(f, w):
                at = SOFTPOS_STEPS * (2 * f + w)
                if w == 0:
                    dve.wait_ge(xe_ready, f + 1)
                    src = xe[:, :, :]
                else:
                    dve.wait_ge(conv_t_ready, f + 1)
                    src = fr[1][:, :].rearrange("p (c k) -> p c k", c=NT)
                nc.vector.reduce_max(ch_max[:, w, :], src, AX_X).then_inc(softpos_step, 1)
                dve.wait_ge(softpos_step, at + 1)
                nc.vector.tensor_tensor(out=shifted[:, :, :], in0=src,
                                        in1=ch_max[:, w, :].unsqueeze(2).to_broadcast([P, NT, P]),
                                        op=ALU.subtract).then_inc(softpos_step, 1)

            def channel_softmax(f, w):
                at = SOFTPOS_STEPS * (2 * f + w)
                dve.wait_ge(ch_exp_ready, 2 * f + (w + 1))
                nc.vector.reduce_sum(ch_sum[:, w, :], ch_exp[:, :, :], AX_X).then_inc(softpos_step, 1)
                dve.wait_ge(softpos_step, at + 3)
                nc.vector.reciprocal(ch_rcp[:, w, :], ch_sum[:, w, :]).then_inc(softpos_step, 1)
                dve.wait_ge(softpos_step, at + 4)
                nc.vector.tensor_tensor(out=sel[:, :, :], in0=ch_exp[:, :, :],
                                        in1=ch_rcp[:, w, :].unsqueeze(2).to_broadcast([P, NT, P]),
                                        op=ALU.mult).then_inc(softpos_step, 1)

            def ln1_stats(blk):
                nc.vector.bn_stats(stats1[:, blk, :], h[:, blk, PAD:]).then_inc(ln1_step, 1)

            def ln1_finish_stats(f):
                dve.wait_ge(ln1_step, LN1_STEPS * f + 4)
                nc.vector.memset(spare[:, :], 0.0)
                for j in range(NT):
                    nc.vector.bn_aggr(mv1[:, j, :], stats1[:, j, :]).then_inc(ln1_step, 1)

            def refine(r, var, root, root_at, step, at):
                dve.wait_ge(root, root_at)
                nc.vector.scalar_tensor_tensor(out=r[2], in0=var, scalar=LN_EPS, in1=r[1], op0=ALU.add,
                                               op1=ALU.mult).then_inc(step, 1)
                dve.wait_ge(step, at + 1)
                nc.vector.scalar_tensor_tensor(out=r[2], in0=r[2], scalar=-0.5, in1=r[1], op0=ALU.mult,
                                               op1=ALU.mult).then_inc(step, 1)
                dve.wait_ge(step, at + 2)
                return nc.vector.scalar_tensor_tensor(out=r[3], in0=r[2], scalar=1.5, in1=r[1], op0=ALU.add,
                                                      op1=ALU.mult)

            def ln1_scale(f):
                at = LN1_STEPS * f
                dve.wait_ge(ln1_step, at + 8)
                refine([rstd1[:, k, :] for k in range(4)], mv1[:, :, 1], ln1_root, 2 * f + 2, ln1_step, at + 8
                       ).then_inc(n_scale_ready, 1)

            def ln1_normalise(f, blocks):
                dve.wait_ge(n_scale_ready, f + 1)
                for j in blocks:
                    nc.vector.tensor_scalar(n[:, j, :], h[:, j, PAD:], mv1[:, j, 0:1], rstd1[:, 3, j:j + 1],
                                            ALU.subtract, ALU.mult).then_inc(n_ready, 1)

            def query_row_terms(f):
                for j in range(NT):
                    dve.wait_ge(n_ready, 4 * f + (j + 1))
                    if j:
                        dve.wait_ge(row_term_ready, 4 * f + j)
                    nc.vector.tensor_tensor_reduce(out=junk[:, :], in0=n[:, j, :], in1=key_row[:, :], scale=1.0,
                                                   scalar=bqbk[:, :], op0=ALU.mult, op1=ALU.add,
                                                   accum_out=row_term[:, j:j + 1]).then_inc(row_term_ready, 1)

            def nt_rest(f, j, bank):
                low(nt_lo[:, j, :], fr[bank][:, :], nt_hi[:, j, :], nt_high, 4 * f + (j + 1), nt_split)

            def query_rest(b, j, bank):
                low(q_lo[:, j, :], mm[bank][:, :], q_hi[:, j, :], q_high, 4 * b + (j + 1), q_split,
                    bias=q_bias[:, j:j + 1])

            def value_rest(b, j):
                low(v_lo[:, j, :], mm[j][:, :], v_hi[:, j, :], v_high, 4 * b + (j + 1), v_split)

            def score_shift(b, j):
                at = 3 * (4 * b + j)
                dve.wait_ge(scores_ready, 4 * b + (j + 1))
                if j == 0:
                    dve.wait_ge(row_term_ready, 4 * b + 4)
                nc.vector.reduce_max(s_max[:, j:j + 1], mm[j][:, :], AX_X).then_inc(shift_step, 1)
                dve.wait_ge(shift_step, at + 1)
                nc.vector.tensor_tensor(out=s_top[:, j:j + 1], in0=s_max[:, j:j + 1], in1=row_term[:, j:j + 1],
                                        op=ALU.add).then_inc(shift_step, 1)
                dve.wait_ge(shift_step, at + 2)
                nc.vector.tensor_scalar(s_bias[:, j:j + 1], row_term[:, j:j + 1], s_top[:, j:j + 1], SCALE,
                                        ALU.subtract, ALU.mult).then_inc(shift_step, 1)

            def prob_rest(b, j, bank):
                low(pt_lo[:, j, :, :].rearrange("p c k -> p (c k)"), tp[bank][:, :],
                    pt_hi[:, j, :, :].rearrange("p c k -> p (c k)"), pt_high, 4 * b + (j + 1), pt_split)

            def add_attention(b, j):
                if j == 0:
                    dve.wait_ge(h_attn_ready, 4 * b + 4)
                dve.wait_ge(prob_ready, 4 * b + (j + 1))
                nc.vector.reciprocal(p_rcp[:, j:j + 1], p_sum[:, j:j + 1]).then_inc(p_rcp_ready, 1)
                dve.wait_ge(p_rcp_ready, 4 * b + (j + 1))
                dve.wait_ge(o_ready, 4 * b + (j + 1))
                nc.vector.scalar_tensor_tensor(out=h1[:, j, :], in0=mm[j][:, :], scalar=p_rcp[:, j:j + 1],
                                               in1=h_attn[:, j, :], op0=ALU.mult, op1=ALU.add
                                               ).then_inc(h1_ready, 1)

            def ln2_stats(b, j):
                at = LN2_STEPS * (4 * b + j)
                dve.wait_ge(h1_ready, 4 * b + (j + 1))
                nc.vector.bn_stats(stats2[:, j, :], h1[:, j, :]).then_inc(ln2_step, 1)
                dve.wait_ge(ln2_step, at + 1)
                nc.vector.memset(spare[:, :], 0.0)
                nc.vector.bn_aggr(mv2[:, j, :], stats2[:, j, :]).then_inc(ln2_step, 1)

            def ln2_normalise(b, j):
                at = LN2_STEPS * (4 * b + j)
                dve.wait_ge(ln2_step, at + 2)
                refine([rstd2[:, k, j:j + 1] for k in range(4)], mv2[:, j, 1:2],
                       ln2_root, 2 * (4 * b + j) + 2, ln2_step, at + 2).then_inc(n2_scale_ready, 1)
                dve.wait_ge(n2_scale_ready, 4 * b + (j + 1))
                nc.vector.tensor_scalar(n2[:, j, :], h1[:, j, :], mv2[:, j, 0:1], rstd2[:, 3, j:j + 1],
                                        ALU.subtract, ALU.mult).then_inc(n2_ready, 1)

            def n2_rest(b, j, bank):
                low(n2t_lo[:, j, :, :].rearrange("p c k -> p (c k)"), tp[bank][:, :],
                    n2t_hi[:, j, :, :].rearrange("p c k -> p (c k)"), n2t_high, 4 * b + (j + 1), n2t_split)

            def add_ffn(b, j, bank):
                if j == 0:
                    dve.wait_ge(y_stored, 64 * b + 64)
                dve.wait_ge(h1_ffn_ready, 4 * b + (j + 1))
                dve.wait_ge(f_ready, 4 * b + (j + 1))
                nc.vector.scalar_tensor_tensor(out=y[:, j, :], in0=mm[bank][:, :], scalar=wscale[:, 0:1],
                                               in1=h1_ffn[:, j, :], op0=ALU.mult, op1=ALU.add
                                               ).then_inc(y_ready, 1)

            dve.sem_inc(y_ready, NT)
            embed(0)
            channel_shift(0, 0)
            channel_softmax(0, 0)
            dve.wait_ge(h_x_ready, 1)
            ln1_stats(X_BLK)
            dve.wait_ge(h_conv_ready, 1)
            ln1_stats(CONV_BLK)
            dve.wait_ge(h_ext_ready, 1)
            ln1_stats(XEXT_BLK)
            channel_shift(0, 1)
            channel_softmax(0, 1)
            dve.wait_ge(h_ext_ready, 2)
            ln1_stats(CEXT_BLK)
            ln1_finish_stats(0)
            ln1_scale(0)
            ln1_normalise(0, range(NT))
            dve.wait_ge(consts_ready, 3)
            dve.wait_ge(attn_loaded, 48)
            for part in range(2):
                for c in range(NT):
                    col = (1 + part) * NT + c
                    nc.vector.tensor_scalar(b_wide[:, part, c, :], ones[:, :], b_qkv_sb[:, col:col + 1], None,
                                            ALU.mult).then_inc(wide_ready, 1)
            for j in range(NT):
                low(m_lo[:, j, :], mm[j][:, :], m_hi[:, j, :], merged_hi, j + 1, merged_split)
            dve.wait_ge(bias_mm_ready, 1)
            nc.vector.tensor_copy(q_bias[:, :], tp[0][:, 0:NT]).then_inc(bias_ready, 1)
            nc.vector.tensor_copy(bqbk[:, :], tp[0][:, NT:NT + 1]).then_inc(bias_ready, 1)
            dve.wait_ge(bias_mm_ready, 2)
            nc.vector.tensor_copy(key_row[:, :], tp[1][:, :]).then_inc(bias_ready, 1)
            for j in range(NT):
                low(vo_lo[:, j, :], mm[j][:, :], vo_hi[:, j, :], merged_hi, NT + j + 1, merged_split)
            dve.wait_ge(bias_mm_ready, 3)
            dve.wait_ge(out_loaded, 48)
            nc.vector.tensor_tensor(out=attn_bias[:, :], in0=fr[0][:, :], in1=b_out_sb[:, :],
                                    op=ALU.add).then_inc(bias_ready, 1)
            dve.wait_ge(ffn_loaded, 32)
            nc.vector.tensor_reduce(wsum[:, :], w_ffn_sb[:, :, :].rearrange("p c t -> p (c t)"), AX_X, ALU.add,
                                    apply_absolute_value=True).then_inc(abs_ready, 1)
            dve.wait_ge(abs_total, 1)
            nc.vector.tensor_scalar(wscale[:, 0:1], fr[1][:, 0:1], 1.0 / (T * T), None, ALU.mult
                                    ).then_inc(tern_step, 1)
            dve.wait_ge(tern_step, 1)
            nc.vector.tensor_scalar(wscale[:, 1:2], wscale[:, 0:1], W_EPS, 0.5, ALU.add, ALU.mult
                                    ).then_inc(tern_step, 1)
            dve.wait_ge(tern_step, 2)
            nc.vector.tensor_scalar(wscale[:, 2:3], wscale[:, 1:2], -1.0, None, ALU.mult).then_inc(tern_step, 1)
            dve.wait_ge(tern_step, 3)
            nc.vector.tensor_scalar(below[:, :, :], w_ffn_sb[:, :, :], wscale[:, 2:3], None, ALU.is_lt
                                    ).then_inc(tern_step, 1)
            dve.wait_ge(tern_step, 4)
            nc.vector.scalar_tensor_tensor(out=tern[:, :, :], in0=w_ffn_sb[:, :, :], scalar=wscale[:, 1:2],
                                           in1=below[:, :, :], op0=ALU.is_gt, op1=ALU.subtract
                                           ).then_inc(tern_ready, 1)
            for j, bank in enumerate((0, 1, 0, 1)):
                nt_rest(0, j, bank)
            dve.wait_ge(bias_ready, 4)
            for j in range(NT):
                query_rest(0, j, j)
            query_row_terms(0)
            embed(1)
            channel_shift(1, 0)
            channel_softmax(1, 0)

            def batch(b, tower, embed_next):
                f = b + 1
                value_rest(b, 0)
                value_rest(b, 1)
                if tower:
                    dve.wait_ge(h_x_ready, f + 1)
                    ln1_stats(X_BLK)
                value_rest(b, 2)
                if tower:
                    channel_shift(f, 1)
                    dve.wait_ge(h_conv_ready, f + 1)
                    ln1_stats(CONV_BLK)
                    channel_softmax(f, 1)
                value_rest(b, 3)
                if tower:
                    dve.wait_ge(h_ext_ready, 2 * f + 1)
                    ln1_stats(XEXT_BLK)
                score_shift(b, 0)
                score_shift(b, 1)
                if tower:
                    dve.wait_ge(h_ext_ready, 2 * f + 2)
                    ln1_stats(CEXT_BLK)
                    ln1_finish_stats(f)
                score_shift(b, 2)
                if tower:
                    ln1_scale(f)
                    ln1_normalise(f, (0, 1))
                prob_rest(b, 0, 0)
                score_shift(b, 3)
                if tower:
                    ln1_normalise(f, (2, 3))
                prob_rest(b, 1, 1)
                add_attention(b, 0)
                ln2_stats(b, 0)
                prob_rest(b, 2, 0)
                ln2_normalise(b, 0)
                add_attention(b, 1)
                ln2_stats(b, 1)
                prob_rest(b, 3, 1)
                if tower:
                    nt_rest(f, 0, 0)
                    nt_rest(f, 1, 1)
                ln2_normalise(b, 1)
                add_attention(b, 2)
                if tower:
                    nt_rest(f, 2, 0)
                    nt_rest(f, 3, 1)
                ln2_stats(b, 2)
                add_attention(b, 3)
                ln2_normalise(b, 2)
                ln2_stats(b, 3)
                if tower:
                    query_rest(f, 0, 0)
                n2_rest(b, 0, 0)
                ln2_normalise(b, 3)
                if tower:
                    query_rest(f, 1, 1)
                n2_rest(b, 1, 1)
                add_ffn(b, 0, 2)
                if embed_next:
                    embed(f + 1)
                    channel_shift(f + 1, 0)
                if tower:
                    query_rest(f, 2, 3)
                n2_rest(b, 2, 0)
                add_ffn(b, 1, 0)
                if tower:
                    query_row_terms(f)
                    query_rest(f, 3, 1)
                n2_rest(b, 3, 1)
                add_ffn(b, 2, 2)
                if embed_next:
                    channel_softmax(f + 1, 0)
                add_ffn(b, 3, 3)

            with dve.Fori(0, B - 2) as b:
                batch(b, True, True)
            batch(B - 2, True, False)
            batch(B - 1, False, False)


def position_table():
    import numpy as np
    depth = P // 2
    times = np.arange(T, dtype=np.float32)[:, None]
    depths = np.arange(depth, dtype=np.float32)[None, :] / np.float32(depth)
    rate = (np.float32(1.0) / np.power(np.float32(10000.0), depths)).astype(np.float32)
    angle = (times * rate).astype(np.float32)
    table = np.concatenate([np.sin(angle), np.cos(angle)], axis=-1).astype(np.float32)
    return np.ascontiguousarray(table.reshape(NT, P, P).transpose(1, 0, 2))


def kernel(x, L0_tok_emb_table, L0_tok_conv_w, L0_tok_conv_b, L0_tok_spos0, L0_tok_spos1, L0_attn_w_qkv,
           L0_attn_b_qkv, L0_attn_w_out, L0_attn_b_out, L0_ffn_weight, L0_ffn_bias):
    import numpy as np
    import concourse.bacc as bacc
    from concourse.bass_utils import run_bass_kernel_spmd

    B = x.shape[0]
    cols = [
        ("ids", np.asarray(x).reshape(B * NT, P).T),
        ("emb", L0_tok_emb_table),
        ("pos", position_table()),
        ("conv_w", np.asarray(L0_tok_conv_w).transpose(1, 2, 0)),
        ("conv_b", np.asarray(L0_tok_conv_b).reshape(P, 1)),
        ("spos0", L0_tok_spos0),
        ("spos1", L0_tok_spos1),
        ("w_qkv", L0_attn_w_qkv),
        ("b_qkv", np.asarray(L0_attn_b_qkv).reshape(3 * NT, P).T),
        ("w_out_t", np.asarray(L0_attn_w_out).T),
        ("b_out", L0_attn_b_out),
        ("w_ffn_t", np.asarray(L0_ffn_weight).T),
        ("b_ffn", L0_ffn_bias),
    ]
    nc = bacc.Bacc("TRN2", target_bir_lowering=False, num_devices=1)
    arrays, args = {}, []
    for name, a in cols:
        a = np.ascontiguousarray(a)
        arrays[f"in_{name}"] = a
        args.append(nc.dram_tensor(f"in_{name}", a.shape, mybir.dt.from_np(a.dtype), kind="ExternalInput").ap())
    args.append(nc.dram_tensor("out_h", (B, T, T), F32, kind="ExternalOutput").ap())
    lm_tower(nc, *args)
    r = run_bass_kernel_spmd(nc, [arrays], core_ids=[0])
    return r.results[0]["out_h"]
```

```python
from contextlib import ExitStack

import concourse.bass as bass
from concourse import mybir

ALU = mybir.AluOpType
ACT = mybir.ActivationFunctionType
F32 = mybir.dt.float32
F16 = mybir.dt.float16
I32 = mybir.dt.int32
U32 = mybir.dt.uint32
AX_X = mybir.AxisListType.X

P = 128
T = 512
NT = T // P
PAD = 2
BLK = 32
TAPS = 3
LN_EPS = 1e-5
W_EPS = 1e-10
W_UP = 64.0
SEL_UP = 1024.0
SCALE = float(T) ** -0.5

X_BLK, XEXT_BLK, CONV_BLK, CEXT_BLK = range(4)

SOFTPOS_STEPS = 5
LN1_STEPS = 11
LN2_STEPS = 5

SCORE_BANK = (0, 1, 2, 3)
FFN_BANK = (4, 5, 0, 1)
QUERY_BANK = (2, 3, 4, 5)
ATTEND_BANK = (0, 1, 2, 3)
VALUE_BANK = (4, 5, 0, 1)

POOL_CHUNKS = (0, 1)
DVE_CHUNKS = (2, 3)


def lm_tower(nc, ids, emb, pos, conv_w, conv_b, spos0, spos1, w_qkv, b_qkv, w_out_t, b_out, w_ffn_t, b_ffn, out):
    B = out.shape[0]
    ctx = ExitStack()
    with ctx:
        def sb(name, shape, dt=F32):
            return ctx.enter_context(nc.sbuf_tensor(name, shape, dt))

        def sem(name):
            return ctx.enter_context(nc.semaphore(name))

        ids_sb = sb("ids_sb", [P, B * NT], I32)
        ident = sb("ident", [P, P])
        ones = sb("ones", [P, P])
        pos_sb = sb("pos_sb", [P, NT, P])
        conv_w_sb = sb("conv_w_sb", [P, TAPS, P])
        conv_b_sb = sb("conv_b_sb", [P, 1])
        spos_sb = sb("spos_sb", [P, 2, P])
        conv_w_hi = sb("conv_w_hi", [P, TAPS, P], F16)
        conv_w_lo = sb("conv_w_lo", [P, TAPS, P], F16)
        spos_hi = sb("spos_hi", [P, 2, P], F16)
        spos_lo = sb("spos_lo", [P, 2, P], F16)
        w_qkv_sb = sb("w_qkv_sb", [P, 3 * NT, T])
        b_qkv_sb = sb("b_qkv_sb", [P, 3 * NT])
        w_out_sb = sb("w_out_sb", [P, NT, T])
        w_ffn_sb = sb("w_ffn_sb", [P, NT, T])
        b_out_sb = sb("b_out_sb", [P, T])
        b_ffn_sb = sb("b_ffn_sb", [P, T])
        b_wide = sb("b_wide", [P, 2, NT, P])
        m_hi = sb("m_hi", [P, NT, T], F16)
        m_lo = sb("m_lo", [P, NT, T], F16)
        vo_hi = sb("vo_hi", [P, NT, T], F16)
        vo_lo = sb("vo_lo", [P, NT, T], F16)
        tern = sb("tern", [P, NT, T], F16)
        q_bias = sb("q_bias", [P, NT])
        key_row = sb("key_row", [P, T])
        bqbk = sb("bqbk", [P, 1])
        attn_bias = sb("attn_bias", [P, T])
        wsum = sb("wsum", [P, 1])
        wscale = sb("wscale", [P, 3])

        idx = sb("idx", [P, NT], I32)
        gathered_sb = sb("gathered_sb", [P, NT, P])
        xe = sb("xe", [P, NT, P])
        ch_max = sb("ch_max", [P, 2, NT])
        ch_sum = sb("ch_sum", [P, 2, NT])
        ch_rcp = sb("ch_rcp", [P, 2, NT])
        shifted = sb("shifted", [P, NT, P])
        ch_exp = sb("ch_exp", [P, NT, P])
        sel = sb("sel", [P, NT, P])
        x_hi = sb("x_hi", [P, PAD + T], F16)
        x_lo = sb("x_lo", [P, PAD + T], F16)
        sel_hi = sb("sel_hi", [P, T], F16)
        sel_lo = sb("sel_lo", [P, T], F16)
        h = sb("h", [P, NT, T])
        h_attn = sb("h_attn", [P, NT, T])
        stats1 = sb("stats1", [P, NT, 6])
        mv1 = sb("mv1", [P, NT, 2])
        rstd1 = sb("rstd1", [P, 5, NT])
        n = sb("n", [P, NT, T])
        junk = sb("junk", [P, T])
        row_term = sb("row_term", [P, NT])
        nt_hi = sb("nt_hi", [P, NT, T], F16)
        nt_lo = sb("nt_lo", [P, NT, T], F16)
        q_hi = sb("q_hi", [P, NT, T], F16)
        q_lo = sb("q_lo", [P, NT, T], F16)
        v_hi = sb("v_hi", [P, NT, T], F16)
        v_lo = sb("v_lo", [P, NT, T], F16)
        s_max = sb("s_max", [P, NT])
        s_top = sb("s_top", [P, NT])
        s_bias = sb("s_bias", [P, NT])
        prob = sb("prob", [P, NT, T])
        p_sum = sb("p_sum", [P, NT])
        p_rcp = sb("p_rcp", [P, NT])
        pt_hi = sb("pt_hi", [P, NT, T], F16)
        pt_lo = sb("pt_lo", [P, NT, T], F16)
        h1 = sb("h1", [P, NT, T])
        h1_ffn = sb("h1_ffn", [P, NT, T])
        stats2 = sb("stats2", [P, NT, 6])
        mv2 = sb("mv2", [P, NT, 2])
        rstd2 = sb("rstd2", [P, 5, NT])
        n2 = sb("n2", [P, NT, T])
        n2t_hi = sb("n2t_hi", [P, NT, T], F16)
        n2t_lo = sb("n2t_lo", [P, NT, T], F16)
        y = sb("y", [P, NT, T])
        below = y
        n_blocks = w_qkv_sb[:, 0:NT, :]
        n_t = w_qkv_sb[:, NT:2 * NT, :]
        p_blocks = w_qkv_sb[:, 2 * NT:, :]
        p_t = prob
        n2_blocks = w_out_sb[:, :, :]
        n2_t = n2
        h1_ffn_last, y_last = h_attn, n
        ln_eps = sb("ln_eps", [P, 1])
        spare = sb("spare", [P, 1])

        mm = [ctx.enter_context(nc.psum_tensor(f"mm{k}", [P, T], F32)) for k in range(6)]
        tp = mm[4:6]
        fr = [ctx.enter_context(nc.psum_tensor(f"fr{k}", [P, T], F32)) for k in range(2)]

        ids_loaded = sem("ids_loaded")
        pos_loaded = sem("pos_loaded")
        tower_loaded = sem("tower_loaded")
        qk_loaded = [sem(f"qk_loaded{c}") for c in range(NT)]
        out_loaded = sem("out_loaded")
        ffn_loaded = sem("ffn_loaded")
        ident_zeroed = sem("ident_zeroed")
        consts_ready = sem("consts_ready")
        pads_zeroed = sem("pads_zeroed")
        wide_ready = sem("wide_ready")
        small_high = sem("small_high")
        small_split = sem("small_split")
        merged_ready = sem("merged_ready")
        merged_hi = sem("merged_hi")
        merged_split = sem("merged_split")
        bias_mm_ready = sem("bias_mm_ready")
        bias_ready = sem("bias_ready")
        abs_ready = sem("abs_ready")
        abs_total = sem("abs_total")
        tern_step = sem("tern_step")
        tern_ready = sem("tern_ready")
        idx_ready = sem("idx_ready")
        rows_gathered = sem("rows_gathered")
        xe_ready = sem("xe_ready")
        x_t_ready = sem("x_t_ready")
        h_x_ready = sem("h_x_ready")
        softpos_step = sem("softpos_step")
        ch_exp_ready = sem("ch_exp_ready")
        sel_t_ready = sem("sel_t_ready")
        sel_high = sem("sel_high")
        sel_split = sem("sel_split")
        x_split = sem("x_split")
        conv_ready = sem("conv_ready")
        h_conv_ready = sem("h_conv_ready")
        conv_t_ready = sem("conv_t_ready")
        ext_ready = sem("ext_ready")
        h_ext_ready = sem("h_ext_ready")
        ln1_step = sem("ln1_step")
        ln1_root = sem("ln1_root")
        n_scale_ready = sem("n_scale_ready")
        n_ready = sem("n_ready")
        n_turned = sem("n_turned")
        n_moved = sem("n_moved")
        row_term_ready = sem("row_term_ready")
        h_attn_ready = sem("h_attn_ready")
        nt_ready, nt_high, nt_split = sem("nt_ready"), sem("nt_high"), sem("nt_split")
        q_ready, q_high, q_split = sem("q_ready"), sem("q_high"), sem("q_split")
        v_ready, v_high, v_split = sem("v_ready"), sem("v_high"), sem("v_split")
        scores_ready = sem("scores_ready")
        shift_step = sem("shift_step")
        prob_ready = sem("prob_ready")
        pt_ready, pt_high, pt_split = sem("pt_ready"), sem("pt_high"), sem("pt_split")
        p_turned = sem("p_turned")
        p_moved = sem("p_moved")
        h1_begun = sem("h1_begun")
        p_rcp_ready = sem("p_rcp_ready")
        o_ready = sem("o_ready")
        h1_ready = sem("h1_ready")
        h1_ffn_ready = sem("h1_ffn_ready")
        ln2_step = sem("ln2_step")
        ln2_root = sem("ln2_root")
        n2_scale_ready = sem("n2_scale_ready")
        n2_ready = sem("n2_ready")
        n2_turned = sem("n2_turned")
        n2_moved = sem("n2_moved")
        n2t_ready, n2t_high, n2t_split = sem("n2t_ready"), sem("n2t_high"), sem("n2t_split")
        f_ready = sem("f_ready")
        y_ready = sem("y_ready")
        y_stored = sem("y_stored")

        def half(j):
            return slice(j * P, (j + 1) * P)

        def chunk(moved, c):
            return moved.rearrange("p i (c j b) -> p c j i b", c=NT, j=NT)[:, c, :, :, :]

        def rows(tile):
            return tile.rearrange("p (j i b) -> p j i b", j=NT, i=NT)

        block = ctx.enter_context(nc.Block())

        @block.sync
        def _(sp):
            sp.sem_inc(y_stored, 64)
            sp.dma_start(ids_sb[:, :], ids).then_inc(ids_loaded, 16)

            def load_qk(c):
                for part in range(2):
                    sp.dma_start(w_qkv_sb[:, part * NT + c, :], w_qkv[part * T + c * P:part * T + (c + 1) * P, :]
                                 ).then_inc(qk_loaded[c], 16)

            load_qk(0)
            sp.dma_start(pos_sb[:, :, :], pos).then_inc(pos_loaded, 16)
            sp.dma_start(conv_w_sb[:, :, :], conv_w).then_inc(tower_loaded, 16)
            sp.dma_start(conv_b_sb[:, :], conv_b).then_inc(tower_loaded, 16)
            sp.dma_start(spos_sb[:, 0, :], spos0).then_inc(tower_loaded, 16)
            sp.dma_start(spos_sb[:, 1, :], spos1).then_inc(tower_loaded, 16)
            sp.dma_start(b_qkv_sb[:, :], b_qkv).then_inc(tower_loaded, 16)
            for c in range(1, NT):
                load_qk(c)
            sp.wait_ge(rows_gathered, 64)
            sp.dma_start(w_qkv_sb[:, 2 * NT:, :],
                         w_qkv[2 * T:, :].rearrange("(c p) t -> p c t", p=P)).then_inc(out_loaded, 16)
            sp.dma_start(w_out_sb[:, :, :], w_out_t.rearrange("(c p) t -> p c t", p=P)).then_inc(out_loaded, 16)
            sp.dma_start(b_out_sb[:, :], b_out.partition_broadcast(P)).then_inc(out_loaded, 16)
            sp.dma_start(w_ffn_sb[:, :, :], w_ffn_t.rearrange("(c p) t -> p c t", p=P)).then_inc(ffn_loaded, 16)
            sp.dma_start(b_ffn_sb[:, :], b_ffn.partition_broadcast(P)).then_inc(ffn_loaded, 16)

            def move_blocks(dst, src, turned, b, moved):
                sp.wait_ge(turned, 4 * b + 4)
                for i in range(NT):
                    for m in range(NT):
                        sp.dma_start(dst[m * BLK:(m + 1) * BLK, i, :], src[i * BLK:(i + 1) * BLK, m, :]
                                     ).then_inc(moved, 16)

            def store_rows(b):
                for j in range(NT):
                    sp.wait_ge(y_ready, 4 * b + (j + 5))
                    sp.dma_start(out[b, half(j), :], y[:, j, :]).then_inc(y_stored, 16)

            def batch(b, prev, tower):
                move_blocks(p_t, p_blocks, p_turned, b, p_moved)
                if prev:
                    store_rows(b - 1)
                if tower:
                    move_blocks(n_t, n_blocks, n_turned, b, n_moved)
                move_blocks(n2_t, n2_blocks, n2_turned, b, n2_moved)

            batch(0, False, True)
            with sp.Fori(1, B - 2) as b:
                batch(b, True, True)
            batch(B - 2, True, False)
            store_rows(B - 2)
            for j in range(NT):
                sp.wait_ge(y_ready, 4 * (B - 1) + (j + 5))
                sp.dma_start(out[B - 1, half(j), :], y_last[:, j, :]).then_inc(y_stored, 16)
            sp.wait_ge(y_stored, 64 * (B + 1))

        @block.gpsimd
        def _(pool):
            nc.gpsimd.memset(ident[:, :], 0.0).then_inc(ident_zeroed, 1)
            nc.gpsimd.memset(x_hi[:, 0:PAD], 0.0).then_inc(pads_zeroed, 1)
            nc.gpsimd.memset(x_lo[:, 0:PAD], 0.0).then_inc(pads_zeroed, 1)
            nc.gpsimd.memset(ones[:, :], 1.0).then_inc(consts_ready, 1)
            nc.gpsimd.memset(ln_eps[:, :], LN_EPS).then_inc(consts_ready, 1)
            pool.wait_ge(ident_zeroed, 1)
            nc.gpsimd.affine_select(out=ident[:, :], in_=ident[:, :], compare_op=ALU.not_equal, fill=1.0,
                                    base=0, pattern=[[-1, P]], channel_multiplier=1).then_inc(consts_ready, 1)
            pool.wait_ge(ids_loaded, 16)

            def take_ids(b):
                nc.gpsimd.tensor_copy(idx[:, :], ids_sb[:, bass.ts(b, NT)]).then_inc(idx_ready, 1)

            def gather():
                for c in range(NT):
                    nc.gpsimd.indirect_dma_start(
                        out=gathered_sb[:, c, :], out_offset=None, in_=emb,
                        in_offset=bass.IndirectOffsetOnAxis(ap=idx[:, c:c + 1], axis=0)
                    ).then_inc(rows_gathered, 16)

            def add_attention_bias(j):
                nc.gpsimd.tensor_tensor(out=h_attn[:, j, :], in0=h[:, j, :], in1=attn_bias[:, :],
                                        op=ALU.add).then_inc(h_attn_ready, 1)

            def add_ffn_bias(b):
                pool.wait_ge(y_ready, 4 * b + 4)
                for j in range(NT):
                    pool.wait_ge(h1_ready, 4 * b + (j + 1))
                    nc.gpsimd.tensor_tensor(out=h1_ffn[:, j, :], in0=h1[:, j, :], in1=b_ffn_sb[:, :],
                                            op=ALU.add).then_inc(h1_ffn_ready, 1)

            take_ids(0)
            pool.wait_ge(idx_ready, 1)
            gather()
            pool.wait_ge(xe_ready, 1)
            pool.wait_ge(rows_gathered, 64)
            take_ids(1)
            pool.wait_ge(idx_ready, 2)
            gather()
            pool.wait_ge(xe_ready, 2)
            pool.wait_ge(rows_gathered, 128)
            take_ids(2)
            pool.wait_ge(idx_ready, 3)
            gather()
            pool.wait_ge(bias_ready, 4)
            pool.wait_ge(ffn_loaded, 32)
            pool.wait_ge(n_ready, 4)
            for j in range(NT):
                add_attention_bias(j)

            def low(dst, src, hi, high_done, at, done):
                pool.wait_ge(high_done, at)
                nc.gpsimd.tensor_tensor(out=rows(dst), in0=src, in1=rows(hi), op=ALU.subtract).then_inc(done, 1)

            def batch(b, prev, gather_next):
                pool.wait_ge(n_ready, 4 * b + 8)
                for j in range(NT - 1):
                    pool.wait_ge(h1_begun, 4 * b + (j + 1))
                    add_attention_bias(j)
                if gather_next:
                    pool.wait_ge(xe_ready, b + 3)
                    take_ids(b + 3)
                    pool.wait_ge(idx_ready, b + 4)
                pool.wait_ge(h1_begun, 4 * b + 4)
                add_attention_bias(NT - 1)
                if prev:
                    for c in POOL_CHUNKS:
                        low(n2t_lo[:, c, :], chunk(n2_t, c), n2t_hi[:, c, :], n2t_high, 4 * b + (c - 3), n2t_split)
                    for c in POOL_CHUNKS:
                        low(nt_lo[:, c, :], chunk(n_t, c), nt_hi[:, c, :], nt_high, 4 * b + (c + 5), nt_split)
                if gather_next:
                    gather()
                for c in POOL_CHUNKS:
                    low(pt_lo[:, c, :], chunk(p_t, c), pt_hi[:, c, :], pt_high, 4 * b + (c + 1), pt_split)
                add_ffn_bias(b)

            batch(0, False, True)
            with pool.Fori(1, B - 3) as b:
                batch(b, True, True)
            batch(B - 3, True, False)
            batch(B - 2, True, False)
            for c in POOL_CHUNKS:
                low(n2t_lo[:, c, :], chunk(n2_t, c), n2t_hi[:, c, :], n2t_high, 4 * (B - 2) + (c + 1), n2t_split)
            for j in range(NT):
                pool.wait_ge(h1_ready, 4 * (B - 1) + (j + 1))
                nc.gpsimd.tensor_tensor(out=h1_ffn_last[:, j, :], in0=h1[:, j, :], in1=b_ffn_sb[:, :],
                                        op=ALU.add).then_inc(h1_ffn_ready, 1)

        @block.tensor
        def _(pe):
            def transpose4(dst, src, done):
                for c in range(NT):
                    last = nc.tensor.transpose(dst[:, half(c)], src(c), ident[:, :])
                last.then_inc(done, 1)

            def split_product(dst, a_hi, a_lo, b_hi, b_lo, done):
                for c in range(NT):
                    nc.tensor.matmul(dst[:, :], a_hi(c), b_hi(c), start=(c == 0), stop=False)
                    nc.tensor.matmul(dst[:, :], a_hi(c), b_lo(c), start=False, stop=False)
                    last = nc.tensor.matmul(dst[:, :], a_lo(c), b_hi(c), start=False, stop=(c == NT - 1))
                last.then_inc(done, 1)

            def x_transpose(f):
                pe.wait_ge(xe_ready, f + 1)
                transpose4(fr[0], lambda c: xe[:, c, :], x_t_ready)

            def sel_transpose(f, w):
                pe.wait_ge(softpos_step, SOFTPOS_STEPS * (2 * f + (w + 1)))
                transpose4(fr[1], lambda c: sel[:, c, :], sel_t_ready)

            def convolution(f):
                pe.wait_ge(x_split, f + 1)
                for k in range(TAPS):
                    nc.tensor.matmul(fr[0][:, :], conv_w_hi[:, k, :], x_hi[:, k:k + T], start=(k == 0), stop=False)
                    nc.tensor.matmul(fr[0][:, :], conv_w_hi[:, k, :], x_lo[:, k:k + T], start=False, stop=False)
                    last = nc.tensor.matmul(fr[0][:, :], conv_w_lo[:, k, :], x_hi[:, k:k + T],
                                            start=False, stop=(k == TAPS - 1))
                last.then_inc(conv_ready, 1)

            def conv_transpose(f):
                pe.wait_ge(h_conv_ready, f + 1)
                transpose4(fr[1], lambda c: h[:, CONV_BLK, half(c)], conv_t_ready)

            def extension(f, w):
                pe.wait_ge(sel_split, 2 * f + (w + 1))
                if w == 0:
                    pe.wait_ge(h_conv_ready, f + 1)
                else:
                    pe.wait_ge(h_ext_ready, 2 * f + 1)
                nc.tensor.matmul(fr[0][:, :], spos_hi[:, w, :], sel_hi[:, :], start=True, stop=False)
                nc.tensor.matmul(fr[0][:, :], spos_hi[:, w, :], sel_lo[:, :], start=False, stop=False)
                nc.tensor.matmul(fr[0][:, :], spos_lo[:, w, :], sel_hi[:, :], start=False, stop=True
                                 ).then_inc(ext_ready, 1)

            def nt_transpose(f, j, bank):
                pe.wait_ge(n_ready, 4 * f + 4)
                transpose4(bank, lambda c: n[:, c, half(j)], nt_ready)

            def queries(b, j):
                pe.wait_ge(nt_split, 4 * b + 4)
                split_product(mm[QUERY_BANK[j]], lambda c: m_hi[:, c, half(j)], lambda c: m_lo[:, c, half(j)],
                              lambda c: nt_hi[:, c, :], lambda c: nt_lo[:, c, :], q_ready)

            def values(b, j):
                split_product(mm[VALUE_BANK[j]], lambda c: nt_hi[:, c, half(j)], lambda c: nt_lo[:, c, half(j)],
                              lambda c: vo_hi[:, c, :], lambda c: vo_lo[:, c, :], v_ready)

            def scores(b, j):
                if j < 2:
                    pe.wait_ge(v_split, 4 * b + (j + 3))
                if j == 0:
                    pe.wait_ge(q_split, 4 * b + 4)
                split_product(mm[SCORE_BANK[j]], lambda c: q_hi[:, c, half(j)], lambda c: q_lo[:, c, half(j)],
                              lambda c: nt_hi[:, c, :], lambda c: nt_lo[:, c, :], scores_ready)

            def prob_transpose(b, j):
                pe.wait_ge(prob_ready, 4 * b + (j + 1))
                if j >= 2:
                    pe.wait_ge(pt_split, 4 * b + (j - 1))
                transpose4(fr[j % 2], lambda c: prob[:, j, half(c)], pt_ready)

            def attend(b, j, split):
                pe.wait_ge(pt_split, split)
                split_product(mm[ATTEND_BANK[j]], lambda c: pt_hi[:, c, half(j)], lambda c: pt_lo[:, c, half(j)],
                              lambda c: v_hi[:, c, :], lambda c: v_lo[:, c, :], o_ready)

            def n2_transpose(b, j):
                pe.wait_ge(n2_ready, 4 * b + (j + 1))
                if j >= 2:
                    pe.wait_ge(n2t_split, 4 * b + (j - 1))
                transpose4(fr[j % 2], lambda c: n2[:, j, half(c)], n2t_ready)

            def ffn(b, j, split):
                pe.wait_ge(n2t_split, split)
                bank = FFN_BANK[j]
                for c in range(NT):
                    nc.tensor.matmul(mm[bank][:, :], n2t_hi[:, c, half(j)], tern[:, c, :],
                                     start=(c == 0), stop=False)
                    last = nc.tensor.matmul(mm[bank][:, :], n2t_lo[:, c, half(j)], tern[:, c, :],
                                            start=False, stop=(c == NT - 1))
                last.then_inc(f_ready, 1)

            def key_query_merge(c):
                pe.wait_ge(qk_loaded[c], 32)
                for j in range(NT):
                    step = nc.tensor.matmul(mm[j][:, :], w_qkv_sb[:, c, half(j)], w_qkv_sb[:, NT + c, :],
                                            start=(c == 0), stop=(c == NT - 1))
                    if c == NT - 1:
                        step.then_inc(merged_ready, 1)

            def value_out_merge(j):
                pe.wait_ge(merged_split, j + 1)
                for c in range(NT):
                    last = nc.tensor.matmul(mm[j][:, :], w_qkv_sb[:, 2 * NT + c, half(j)], w_out_sb[:, c, :],
                                            start=(c == 0), stop=(c == NT - 1))
                last.then_inc(merged_ready, 1)

            key_query_merge(0)
            pe.wait_ge(consts_ready, 3)
            pe.wait_ge(pads_zeroed, 2)
            key_query_merge(1)
            x_transpose(0)
            key_query_merge(2)
            sel_transpose(0, 0)
            pe.wait_ge(small_split, 2)
            convolution(0)
            key_query_merge(3)
            extension(0, 0)
            conv_transpose(0)
            pe.wait_ge(out_loaded, 48)
            value_out_merge(0)
            pe.wait_ge(wide_ready, 8)
            for j in range(NT):
                for c in range(NT):
                    nc.tensor.matmul(tp[0][:, j:j + 1], w_qkv_sb[:, NT + c, half(j)], b_qkv_sb[:, c:c + 1],
                                     start=(c == 0), stop=(c == NT - 1))
            for c in range(NT):
                last = nc.tensor.matmul(tp[0][:, NT:NT + 1], b_wide[:, 0, c, :], b_qkv_sb[:, c:c + 1],
                                        start=(c == 0), stop=(c == NT - 1))
            last.then_inc(bias_mm_ready, 1)
            sel_transpose(0, 1)
            value_out_merge(1)
            extension(0, 1)
            value_out_merge(2)
            for c in range(NT):
                last = nc.tensor.matmul(tp[1][:, :], b_wide[:, 0, c, :], w_qkv_sb[:, c, :],
                                        start=(c == 0), stop=(c == NT - 1))
            last.then_inc(bias_mm_ready, 1)
            pe.wait_ge(h_ext_ready, 2)
            nt_transpose(0, 0, fr[0])
            nt_transpose(0, 1, fr[1])
            value_out_merge(3)
            pe.wait_ge(nt_split, 2)
            nt_transpose(0, 2, fr[0])
            nt_transpose(0, 3, fr[1])
            pe.wait_ge(bias_ready, 3)
            for c in range(NT):
                last = nc.tensor.matmul(tp[0][:, :], b_wide[:, 1, c, :], w_out_sb[:, c, :],
                                        start=(c == 0), stop=(c == NT - 1))
            last.then_inc(bias_mm_ready, 1)
            pe.wait_ge(abs_ready, 1)
            nc.tensor.matmul(tp[1][:, 0:1], ones[:, :], wsum[:, :], start=True, stop=True).then_inc(abs_total, 1)
            pe.wait_ge(merged_split, 2 * NT)
            queries(0, 0)
            x_transpose(1)
            queries(0, 1)
            sel_transpose(1, 0)
            pe.wait_ge(bias_ready, 4)
            queries(0, 2)
            convolution(1)
            pe.wait_ge(tern_step, 1)
            queries(0, 3)
            extension(1, 0)
            conv_transpose(1)
            pe.wait_ge(q_split, 3)
            values(0, 0)
            pe.wait_ge(q_split, 4)
            values(0, 1)
            sel_transpose(1, 1)
            values(0, 2)
            extension(1, 1)
            values(0, 3)
            pe.wait_ge(tern_ready, 1)

            def batch(b, prev, tower):
                f, g = b + 1, b + 2
                scores(b, 0)
                if tower:
                    pe.wait_ge(h_ext_ready, 2 * g)
                    x_transpose(g)
                scores(b, 1)
                if tower:
                    sel_transpose(g, 0)
                scores(b, 2)
                scores(b, 3)
                if not prev:
                    pe.wait_ge(x_split, g + 1)
                    pe.wait_ge(sel_split, 2 * g + 1)
                    for j in range(NT):
                        nt_transpose(f, j, (fr + tp)[j])
                    pe.wait_ge(nt_split, 4 * f + 2)
                if tower:
                    convolution(g)
                if prev:
                    ffn(b - 1, 0, 4 * b)
                    ffn(b - 1, 1, 4 * b)
                if tower and prev:
                    extension(g, 0)
                    conv_transpose(g)
                if prev:
                    pe.wait_ge(prob_ready, 4 * b + 1)
                    ffn(b - 1, 2, 4 * b)
                if prev:
                    pe.wait_ge(prob_ready, 4 * b + 2)
                    ffn(b - 1, 3, 4 * b)
                pe.wait_ge(prob_ready, 4 * b + 3)
                queries(f, 0)
                if not prev:
                    extension(g, 0)
                    conv_transpose(g)
                if tower and prev:
                    sel_transpose(g, 1)
                pe.wait_ge(prob_ready, 4 * b + 4)
                queries(f, 1)
                if not prev:
                    sel_transpose(g, 1)
                if tower and prev:
                    extension(g, 1)
                if prev:
                    pe.wait_ge(y_ready, 4 * b + 1)
                queries(f, 2)
                if not prev:
                    extension(g, 1)
                if prev:
                    pe.wait_ge(y_ready, 4 * b + 2)
                queries(f, 3)
                if prev:
                    pe.wait_ge(y_ready, 4 * b + 3)
                attend(b, 0, 4 * b + 4)
                if prev:
                    pe.wait_ge(y_ready, 4 * b + 4)
                attend(b, 1, 4 * b + 4)
                pe.wait_ge(q_split, 4 * f + 1)
                attend(b, 2, 4 * b + 4)
                pe.wait_ge(q_split, 4 * f + 2)
                attend(b, 3, 4 * b + 4)
                pe.wait_ge(q_split, 4 * f + 3)
                values(f, 0)
                pe.wait_ge(q_split, 4 * f + 4)
                values(f, 1)
                pe.wait_ge(h1_ready, 4 * b + 1)
                values(f, 2)
                pe.wait_ge(h1_ready, 4 * b + 2)
                values(f, 3)

            batch(0, False, True)
            with pe.Fori(1, B - 2) as b:
                batch(b, True, True)
            batch(B - 2, True, False)

            last, before = B - 1, B - 2
            scores(last, 0)
            scores(last, 1)
            scores(last, 2)
            prob_transpose(last, 0)
            scores(last, 3)
            prob_transpose(last, 1)
            attend(last, 0, 4 * last + 1)
            prob_transpose(last, 2)
            attend(last, 1, 4 * last + 2)
            prob_transpose(last, 3)
            attend(last, 2, 4 * last + 3)
            attend(last, 3, 4 * last + 4)
            ffn(before, 0, 4 * last)
            ffn(before, 1, 4 * last)
            n2_transpose(last, 0)
            pe.wait_ge(h1_ready, 4 * last + 1)
            ffn(before, 2, 4 * last)
            n2_transpose(last, 1)
            pe.wait_ge(h1_ready, 4 * last + 2)
            ffn(before, 3, 4 * last)
            for j in range(NT):
                if j < 2:
                    n2_transpose(last, j + 2)
                pe.wait_ge(y_ready, 4 * before + (j + 5))
                ffn(last, j, 4 * last + (j + 1))

        @block.scalar
        def _(act):
            def high(dst, src, ready, ready_at, done, bias=None):
                act.wait_ge(ready, ready_at)
                if bias is None:
                    nc.scalar.activation(dst, src, ACT.Copy).then_inc(done, 1)
                else:
                    nc.scalar.activation(dst, src, ACT.Identity, bias=bias).then_inc(done, 1)

            def channel_exp(f, w):
                act.wait_ge(softpos_step, SOFTPOS_STEPS * (2 * f + w) + 2)
                nc.scalar.activation(ch_exp[:, :, :], shifted[:, :, :], ACT.Exp).then_inc(ch_exp_ready, 1)

            def store_x(f):
                act.wait_ge(x_t_ready, f + 1)
                nc.scalar.activation(x_hi[:, PAD:], fr[0][:, :], ACT.Copy)
                if not (isinstance(f, int) and f == 0):
                    act.wait_ge(h_attn_ready, 4 * f - 3)
                nc.scalar.activation(h[:, X_BLK, :], fr[0][:, :], ACT.Copy).then_inc(h_x_ready, 1)

            def sel_half(f, w):
                act.wait_ge(sel_t_ready, 2 * f + (w + 1))
                nc.scalar.activation(sel_hi[:, :], fr[1][:, :], ACT.Copy, scale=SEL_UP).then_inc(sel_high, 1)

            def store_conv(f):
                act.wait_ge(conv_ready, f + 1)
                if not (isinstance(f, int) and f == 0):
                    act.wait_ge(h_attn_ready, 4 * f)
                nc.scalar.activation(h[:, CONV_BLK, :], fr[0][:, :], ACT.Identity, bias=conv_b_sb[:, :],
                                     scale=1.0 / W_UP).then_inc(h_conv_ready, 1)

            def store_ext(f, w):
                act.wait_ge(ext_ready, 2 * f + (w + 1))
                blk = XEXT_BLK if w == 0 else CEXT_BLK
                nc.scalar.activation(h[:, blk, :], fr[0][:, :], ACT.Copy, scale=1.0 / (W_UP * SEL_UP)
                                     ).then_inc(h_ext_ready, 1)

            def rsqrt_guess(out_ln, out_rs, var, ready, ready_at, done, done_at):
                act.wait_ge(ready, ready_at)
                nc.scalar.activation(out_ln, var, ACT.Ln, bias=ln_eps[:, :]).then_inc(done, 1)
                act.wait_ge(done, done_at)
                nc.scalar.activation(out_rs, out_ln, ACT.Exp, scale=-0.5).then_inc(done, 1)

            def ln1_guess(f):
                rsqrt_guess(rstd1[:, 0, :], rstd1[:, 1, :], mv1[:, :, 1], ln1_step, LN1_STEPS * f + 8,
                            ln1_root, 2 * f + 1)

            def ln2_guess(b, j):
                rsqrt_guess(rstd2[:, 0, j:j + 1], rstd2[:, 1, j:j + 1], mv2[:, j, 1:2],
                            ln2_step, LN2_STEPS * (4 * b + j) + 2, ln2_root, 2 * (4 * b + j) + 1)

            def nt_half(f, j, bank):
                high(nt_hi[:, j, :], bank[:, :], nt_ready, 4 * f + (j + 1), nt_high)

            def ln1_normalise(f, blocks):
                act.wait_ge(n_scale_ready, f + 1)
                for j in blocks:
                    nc.scalar.activation(n[:, j, :], h[:, j, :], ACT.Identity, bias=rstd1[:, 4, j:j + 1],
                                         scale=rstd1[:, 3, j:j + 1]).then_inc(n_ready, 1)

            def ln2_normalise(b, j):
                act.wait_ge(n2_scale_ready, 4 * b + (j + 1))
                nc.scalar.activation(n2[:, j, :], h1[:, j, :], ACT.Identity, bias=rstd2[:, 4, j:j + 1],
                                     scale=rstd2[:, 3, j:j + 1]).then_inc(n2_ready, 1)

            def nt_half_moved(b, c):
                high(rows(nt_hi[:, c, :]), chunk(n_t, c), n_moved, 256 * b, nt_high)

            def pt_half_moved(b, c):
                high(rows(pt_hi[:, c, :]), chunk(p_t, c), p_moved, 256 * b + 256, pt_high)

            def n2t_half_moved(b, c):
                high(rows(n2t_hi[:, c, :]), chunk(n2_t, c), n2_moved, 256 * b + 256, n2t_high)

            def query_half(b, j):
                high(q_hi[:, j, :], mm[QUERY_BANK[j]][:, :], q_ready, 4 * b + (j + 1), q_high,
                     bias=q_bias[:, j:j + 1])

            def value_half(b, j):
                high(v_hi[:, j, :], mm[VALUE_BANK[j]][:, :], v_ready, 4 * b + (j + 1), v_high)

            def score_exp(b, j):
                act.wait_ge(shift_step, 3 * (4 * b + j) + 3)
                nc.scalar.activation(prob[:, j, :], mm[SCORE_BANK[j]][:, :], ACT.Exp, bias=s_bias[:, j:j + 1],
                                     scale=SCALE, accum_out=p_sum[:, j:j + 1]).then_inc(prob_ready, 1)

            def prob_half(b, j):
                high(pt_hi[:, :, half(j)], fr[j % 2][:, :].rearrange("p (c k) -> p c k", c=NT),
                     pt_ready, j + 1, pt_high)

            def n2_half(b, j):
                act.wait_ge(f_ready, 4 * b + (j - 3))
                high(n2t_hi[:, :, half(j)], fr[j % 2][:, :].rearrange("p (c k) -> p c k", c=NT),
                     n2t_ready, j + 1, n2t_high)

            act.wait_ge(consts_ready, 3)
            nc.scalar.preload_act_table_set("natural_log_exp_and_others")
            act.wait_ge(tower_loaded, 80)
            nc.scalar.activation(conv_w_hi[:, :, :], conv_w_sb[:, :, :], ACT.Copy, scale=W_UP
                                 ).then_inc(small_high, 1)
            nc.scalar.activation(spos_hi[:, :, :], spos_sb[:, :, :], ACT.Copy, scale=W_UP).then_inc(small_high, 1)

            def merged_half(dst, j, at):
                high(dst[:, j, :], mm[j][:, :], merged_ready, at + j + 1, merged_hi)

            channel_exp(0, 0)
            store_x(0)
            sel_half(0, 0)
            store_conv(0)
            for j in range(NT):
                merged_half(m_hi, j, 0)
            store_ext(0, 0)
            channel_exp(0, 1)
            merged_half(vo_hi, 0, NT)
            sel_half(0, 1)
            merged_half(vo_hi, 1, NT)
            store_ext(0, 1)
            ln1_guess(0)
            ln1_normalise(0, range(NT))
            merged_half(vo_hi, 2, NT)
            nt_half(0, 0, fr[0])
            nt_half(0, 1, fr[1])
            merged_half(vo_hi, 3, NT)
            nt_half(0, 2, fr[0])
            nt_half(0, 3, fr[1])
            channel_exp(1, 0)
            act.wait_ge(bias_ready, 2)
            query_half(0, 0)
            store_x(1)
            query_half(0, 1)
            sel_half(1, 0)
            query_half(0, 2)
            store_conv(1)
            query_half(0, 3)
            store_ext(1, 0)
            channel_exp(1, 1)
            value_half(0, 0)
            sel_half(1, 1)
            value_half(0, 1)
            value_half(0, 2)
            store_ext(1, 1)
            ln1_guess(1)
            value_half(0, 3)
            ln1_normalise(1, range(NT))
            channel_exp(2, 0)

            def begin_h1(b):
                act.wait_ge(h_attn_ready, 4 * b + 4)
                for j in range(NT):
                    nc.scalar.activation(h1[:, j, :], h_attn[:, j, :], ACT.Copy).then_inc(h1_begun, 1)

            def batch(b, prev, tower, embed_next):
                f, g = b + 1, b + 2
                if prev:
                    act.wait_ge(h1_ffn_ready, 4 * b)
                    act.wait_ge(n2_ready, 4 * b)
                begin_h1(b)
                if tower:
                    store_x(g)
                score_exp(b, 0)
                if tower:
                    sel_half(g, 0)
                score_exp(b, 1)
                if prev:
                    for c in range(NT):
                        n2t_half_moved(b - 1, c)
                score_exp(b, 2)
                score_exp(b, 3)
                if tower and prev:
                    store_conv(g)
                for c in range(NT):
                    if prev:
                        nt_half_moved(b, c)
                    else:
                        nt_half(f, c, (fr + tp)[c])
                if tower and not prev:
                    store_conv(g)
                if tower:
                    store_ext(g, 0)
                    channel_exp(g, 1)
                query_half(f, 0)
                if tower:
                    sel_half(g, 1)
                query_half(f, 1)
                if tower:
                    store_ext(g, 1)
                for c in range(NT):
                    pt_half_moved(b, c)
                if tower:
                    ln1_guess(g)
                query_half(f, 2)
                if tower:
                    ln1_normalise(g, (0,))
                query_half(f, 3)
                if tower:
                    ln1_normalise(g, (1, 2, 3))
                ln2_guess(b, 0)
                ln2_normalise(b, 0)
                ln2_guess(b, 1)
                ln2_normalise(b, 1)
                ln2_guess(b, 2)
                ln2_normalise(b, 2)
                ln2_guess(b, 3)
                value_half(f, 0)
                ln2_normalise(b, 3)
                value_half(f, 1)
                value_half(f, 2)
                value_half(f, 3)
                if embed_next:
                    channel_exp(g + 1, 0)

            batch(0, False, True, True)
            with act.Fori(1, B - 3) as b:
                batch(b, True, True, True)
            batch(B - 3, True, True, False)
            batch(B - 2, True, False, False)

            last, before = B - 1, B - 2
            act.wait_ge(h1_ffn_ready, 4 * last)
            act.wait_ge(n2_ready, 4 * last)
            begin_h1(last)
            score_exp(last, 0)
            score_exp(last, 1)
            score_exp(last, 2)
            prob_half(last, 0)
            score_exp(last, 3)
            prob_half(last, 1)
            for c in range(NT):
                n2t_half_moved(before, c)
            prob_half(last, 2)
            prob_half(last, 3)
            ln2_guess(last, 0)
            act.wait_ge(n2t_split, 4 * last)
            ln2_normalise(last, 0)
            ln2_guess(last, 1)
            ln2_normalise(last, 1)
            ln2_guess(last, 2)
            ln2_normalise(last, 2)
            n2_half(last, 0)
            ln2_guess(last, 3)
            ln2_normalise(last, 3)
            for j in range(1, NT):
                n2_half(last, j)

        @block.vector
        def _(dve):
            def low(dst, src, hi, high_done, at, done, bias=None):
                dve.wait_ge(high_done, at)
                if bias is None:
                    nc.vector.tensor_tensor(out=dst, in0=src, in1=hi, op=ALU.subtract).then_inc(done, 1)
                else:
                    nc.vector.scalar_tensor_tensor(out=dst, in0=src, scalar=bias, in1=hi, op0=ALU.add,
                                                   op1=ALU.subtract).then_inc(done, 1)

            def embed(f):
                dve.wait_ge(rows_gathered, 64 * (f + 1))
                if isinstance(f, int) and f == 0:
                    dve.wait_ge(pos_loaded, 16)
                nc.vector.scalar_tensor_tensor(out=xe[:, :, :], in0=gathered_sb[:, :, :], scalar=float(P) ** 0.5,
                                               in1=pos_sb[:, :, :], op0=ALU.mult, op1=ALU.add).then_inc(xe_ready, 1)

            def channel_shift(f, w):
                at = SOFTPOS_STEPS * (2 * f + w)
                if w == 0:
                    dve.wait_ge(xe_ready, f + 1)
                    src = xe[:, :, :]
                else:
                    dve.wait_ge(conv_t_ready, f + 1)
                    src = fr[1][:, :].rearrange("p (c k) -> p c k", c=NT)
                nc.vector.reduce_max(ch_max[:, w, :], src, AX_X).then_inc(softpos_step, 1)
                dve.wait_ge(softpos_step, at + 1)
                nc.vector.tensor_tensor(out=shifted[:, :, :], in0=src,
                                        in1=ch_max[:, w, :].unsqueeze(2).to_broadcast([P, NT, P]),
                                        op=ALU.subtract).then_inc(softpos_step, 1)

            def channel_softmax(f, w):
                at = SOFTPOS_STEPS * (2 * f + w)
                dve.wait_ge(ch_exp_ready, 2 * f + (w + 1))
                nc.vector.reduce_sum(ch_sum[:, w, :], ch_exp[:, :, :], AX_X).then_inc(softpos_step, 1)
                dve.wait_ge(softpos_step, at + 3)
                nc.vector.reciprocal(ch_rcp[:, w, :], ch_sum[:, w, :]).then_inc(softpos_step, 1)
                dve.wait_ge(softpos_step, at + 4)
                nc.vector.tensor_tensor(out=sel[:, :, :], in0=ch_exp[:, :, :],
                                        in1=ch_rcp[:, w, :].unsqueeze(2).to_broadcast([P, NT, P]),
                                        op=ALU.mult).then_inc(softpos_step, 1)

            def x_rest(f):
                low(x_lo[:, PAD:], fr[0][:, :], x_hi[:, PAD:], h_x_ready, f + 1, x_split)

            def sel_rest(f, w):
                dve.wait_ge(sel_high, 2 * f + (w + 1))
                nc.vector.scalar_tensor_tensor(out=sel_lo[:, :], in0=fr[1][:, :], scalar=SEL_UP, in1=sel_hi[:, :],
                                               op0=ALU.mult, op1=ALU.subtract).then_inc(sel_split, 1)

            def ln1_stats(blk):
                nc.vector.bn_stats(stats1[:, blk, :], h[:, blk, :]).then_inc(ln1_step, 1)

            def ln1_finish_stats(f):
                dve.wait_ge(ln1_step, LN1_STEPS * f + 4)
                nc.vector.memset(spare[:, :], 0.0)
                for j in range(NT):
                    nc.vector.bn_aggr(mv1[:, j, :], stats1[:, j, :]).then_inc(ln1_step, 1)

            def refine(r, var, root, root_at, step, at):
                dve.wait_ge(root, root_at)
                nc.vector.scalar_tensor_tensor(out=r[2], in0=var, scalar=LN_EPS, in1=r[1], op0=ALU.add,
                                               op1=ALU.mult).then_inc(step, 1)
                dve.wait_ge(step, at + 1)
                nc.vector.scalar_tensor_tensor(out=r[2], in0=r[2], scalar=-0.5, in1=r[1], op0=ALU.mult,
                                               op1=ALU.mult).then_inc(step, 1)
                dve.wait_ge(step, at + 2)
                return nc.vector.scalar_tensor_tensor(out=r[3], in0=r[2], scalar=1.5, in1=r[1], op0=ALU.add,
                                                      op1=ALU.mult)

            def ln1_scale(f):
                at = LN1_STEPS * f
                dve.wait_ge(ln1_step, at + 8)
                refine([rstd1[:, k, :] for k in range(4)], mv1[:, :, 1], ln1_root, 2 * f + 2, ln1_step, at + 8
                       ).then_inc(ln1_step, 1)
                dve.wait_ge(ln1_step, at + 11)
                nc.vector.scalar_tensor_tensor(out=rstd1[:, 4, :], in0=mv1[:, :, 0], scalar=-1.0,
                                               in1=rstd1[:, 3, :], op0=ALU.mult, op1=ALU.mult
                                               ).then_inc(n_scale_ready, 1)

            def query_row_terms(b, tiles):
                for j in tiles:
                    if j == 0:
                        dve.wait_ge(n_ready, 4 * b + 4)
                    else:
                        dve.wait_ge(row_term_ready, 4 * b + j)
                    nc.vector.tensor_tensor_reduce(out=junk[:, :], in0=n[:, j, :], in1=key_row[:, :], scale=1.0,
                                                   scalar=bqbk[:, :], op0=ALU.mult, op1=ALU.add,
                                                   accum_out=row_term[:, j:j + 1]).then_inc(row_term_ready, 1)

            def nt_rest(f, j, bank):
                low(nt_lo[:, j, :], bank[:, :], nt_hi[:, j, :], nt_high, 4 * f + (j + 1), nt_split)

            def turn_blocks(dst, src, j, ready, ready_at, turned):
                dve.wait_ge(ready, ready_at)
                nc.vector.transpose(dst.rearrange("p m (c j b) -> p j c m b", c=NT, j=NT)[:, j, :, :, :].bitcast(U32),
                                    src[:, j, :].rearrange("p (c m a) -> p c m a", c=NT, m=NT).bitcast(U32)
                                    ).then_inc(turned, 1)

            def turn_n(b, j):
                turn_blocks(n_blocks, n, j, n_ready, 4 * b + (j + 1), n_turned)

            def turn_p(b, j):
                turn_blocks(p_blocks, prob, j, prob_ready, 4 * b + (j + 1), p_turned)

            def turn_n2(b, j):
                turn_blocks(n2_blocks, n2, j, n2_ready, 4 * b + (j + 1), n2_turned)

            def nt_rest_moved(b, c):
                low(rows(nt_lo[:, c, :]), chunk(n_t, c), rows(nt_hi[:, c, :]), nt_high, 4 * b + (c + 5), nt_split)

            def pt_rest_moved(b, c):
                low(rows(pt_lo[:, c, :]), chunk(p_t, c), rows(pt_hi[:, c, :]), pt_high, 4 * b + (c + 1), pt_split)

            def n2t_rest_moved(b, c):
                low(rows(n2t_lo[:, c, :]), chunk(n2_t, c), rows(n2t_hi[:, c, :]), n2t_high, 4 * b + (c + 1), n2t_split)

            def query_rest(b, j):
                low(q_lo[:, j, :], mm[QUERY_BANK[j]][:, :], q_hi[:, j, :], q_high, 4 * b + (j + 1), q_split,
                    bias=q_bias[:, j:j + 1])

            def value_rest(b, j):
                low(v_lo[:, j, :], mm[VALUE_BANK[j]][:, :], v_hi[:, j, :], v_high, 4 * b + (j + 1), v_split)

            def score_shift(b, j):
                at = 3 * (4 * b + j)
                dve.wait_ge(scores_ready, 4 * b + (j + 1))
                if j == 0:
                    dve.wait_ge(row_term_ready, 4 * b + 4)
                nc.vector.reduce_max(s_max[:, j:j + 1], mm[SCORE_BANK[j]][:, :], AX_X).then_inc(shift_step, 1)
                dve.wait_ge(shift_step, at + 1)
                nc.vector.tensor_tensor(out=s_top[:, j:j + 1], in0=s_max[:, j:j + 1], in1=row_term[:, j:j + 1],
                                        op=ALU.add).then_inc(shift_step, 1)
                dve.wait_ge(shift_step, at + 2)
                nc.vector.tensor_scalar(s_bias[:, j:j + 1], row_term[:, j:j + 1], s_top[:, j:j + 1], SCALE,
                                        ALU.subtract, ALU.mult).then_inc(shift_step, 1)

            def prob_rest(b, j):
                low(pt_lo[:, :, half(j)], fr[j % 2][:, :].rearrange("p (c k) -> p c k", c=NT),
                    pt_hi[:, :, half(j)], pt_high, 4 * b + (j + 1), pt_split)

            def add_attention(b, j):
                nc.vector.reciprocal(p_rcp[:, j:j + 1], p_sum[:, j:j + 1]).then_inc(p_rcp_ready, 1)
                dve.wait_ge(h1_begun, 4 * b + (j + 1))
                dve.wait_ge(p_rcp_ready, 4 * b + (j + 1))
                dve.wait_ge(o_ready, 4 * b + (j + 1))
                nc.vector.scalar_tensor_tensor(out=h1[:, j, :], in0=mm[ATTEND_BANK[j]][:, :],
                                               scalar=p_rcp[:, j:j + 1], in1=h1[:, j, :], op0=ALU.mult,
                                               op1=ALU.add).then_inc(h1_ready, 1)

            def ln2_stats(b, j):
                at = LN2_STEPS * (4 * b + j)
                dve.wait_ge(h1_ready, 4 * b + (j + 1))
                nc.vector.bn_stats(stats2[:, j, :], h1[:, j, :]).then_inc(ln2_step, 1)
                dve.wait_ge(ln2_step, at + 1)
                nc.vector.memset(spare[:, :], 0.0)
                nc.vector.bn_aggr(mv2[:, j, :], stats2[:, j, :]).then_inc(ln2_step, 1)

            def ln2_scale(b, j):
                at = LN2_STEPS * (4 * b + j)
                dve.wait_ge(ln2_step, at + 2)
                refine([rstd2[:, k, j:j + 1] for k in range(4)], mv2[:, j, 1:2],
                       ln2_root, 2 * (4 * b + j) + 2, ln2_step, at + 2).then_inc(ln2_step, 1)
                dve.wait_ge(ln2_step, at + 5)
                nc.vector.scalar_tensor_tensor(out=rstd2[:, 4, j:j + 1], in0=mv2[:, j, 0:1], scalar=-1.0,
                                               in1=rstd2[:, 3, j:j + 1], op0=ALU.mult, op1=ALU.mult
                                               ).then_inc(n2_scale_ready, 1)

            def n2_rest(b, j):
                low(n2t_lo[:, :, half(j)], fr[j % 2][:, :].rearrange("p (c k) -> p c k", c=NT),
                    n2t_hi[:, :, half(j)], n2t_high, 4 * b + (j + 1), n2t_split)

            def add_ffn(b, j, h1_bias=h1_ffn, y=y):
                if j == 0 and y is not y_last:
                    dve.wait_ge(y_stored, 64 * b + 64)
                dve.wait_ge(h1_ffn_ready, 4 * b + (j + 1))
                dve.wait_ge(f_ready, 4 * b + (j + 1))
                nc.vector.scalar_tensor_tensor(out=y[:, j, :], in0=mm[FFN_BANK[j]][:, :], scalar=wscale[:, 0:1],
                                               in1=h1_bias[:, j, :], op0=ALU.mult, op1=ALU.add
                                               ).then_inc(y_ready, 1)

            dve.sem_inc(y_ready, NT)
            def merged_rest(dst, dst_hi, j, at):
                low(dst[:, j, :], mm[j][:, :], dst_hi[:, j, :], merged_hi, at + j + 1, merged_split)

            embed(0)
            channel_shift(0, 0)
            dve.wait_ge(consts_ready, 3)
            dve.wait_ge(tower_loaded, 80)
            dve.wait_ge(small_high, 2)
            nc.vector.scalar_tensor_tensor(out=conv_w_lo[:, :, :], in0=conv_w_sb[:, :, :], scalar=W_UP,
                                           in1=conv_w_hi[:, :, :], op0=ALU.mult, op1=ALU.subtract
                                           ).then_inc(small_split, 1)
            nc.vector.scalar_tensor_tensor(out=spos_lo[:, :, :], in0=spos_sb[:, :, :], scalar=W_UP,
                                           in1=spos_hi[:, :, :], op0=ALU.mult, op1=ALU.subtract
                                           ).then_inc(small_split, 1)
            channel_softmax(0, 0)
            x_rest(0)
            sel_rest(0, 0)
            for part in range(2):
                for c in range(NT):
                    col = (1 + part) * NT + c
                    nc.vector.tensor_scalar(b_wide[:, part, c, :], ones[:, :], b_qkv_sb[:, col:col + 1], None,
                                            ALU.mult).then_inc(wide_ready, 1)
            ln1_stats(X_BLK)
            dve.wait_ge(h_conv_ready, 1)
            ln1_stats(CONV_BLK)
            for j in range(NT):
                merged_rest(m_lo, m_hi, j, 0)
            channel_shift(0, 1)
            dve.wait_ge(h_ext_ready, 1)
            ln1_stats(XEXT_BLK)
            channel_softmax(0, 1)
            merged_rest(vo_lo, vo_hi, 0, NT)
            sel_rest(0, 1)
            dve.wait_ge(bias_mm_ready, 1)
            nc.vector.tensor_copy(q_bias[:, :], tp[0][:, 0:NT]).then_inc(bias_ready, 1)
            nc.vector.tensor_copy(bqbk[:, :], tp[0][:, NT:NT + 1]).then_inc(bias_ready, 1)
            dve.wait_ge(ffn_loaded, 32)
            nc.vector.tensor_reduce(wsum[:, :], w_ffn_sb[:, :, :].rearrange("p c t -> p (c t)"), AX_X, ALU.add,
                                    apply_absolute_value=True).then_inc(abs_ready, 1)
            merged_rest(vo_lo, vo_hi, 1, NT)
            dve.wait_ge(h_ext_ready, 2)
            ln1_stats(CEXT_BLK)
            ln1_finish_stats(0)
            ln1_scale(0)
            merged_rest(vo_lo, vo_hi, 2, NT)
            dve.wait_ge(bias_mm_ready, 2)
            nc.vector.tensor_copy(key_row[:, :], tp[1][:, :]).then_inc(bias_ready, 1)
            nt_rest(0, 0, fr[0])
            nt_rest(0, 1, fr[1])
            embed(1)
            channel_shift(1, 0)
            merged_rest(vo_lo, vo_hi, 3, NT)
            nt_rest(0, 2, fr[0])
            nt_rest(0, 3, fr[1])
            channel_softmax(1, 0)
            dve.wait_ge(bias_mm_ready, 3)
            dve.wait_ge(out_loaded, 48)
            nc.vector.tensor_tensor(out=attn_bias[:, :], in0=tp[0][:, :], in1=b_out_sb[:, :],
                                    op=ALU.add).then_inc(bias_ready, 1)
            dve.wait_ge(abs_total, 1)
            nc.vector.tensor_scalar(wscale[:, 0:1], tp[1][:, 0:1], 1.0 / (T * T), None, ALU.mult
                                    ).then_inc(tern_step, 1)
            dve.wait_ge(tern_step, 1)
            nc.vector.tensor_scalar(wscale[:, 1:2], wscale[:, 0:1], W_EPS, 0.5, ALU.add, ALU.mult
                                    ).then_inc(tern_step, 1)
            dve.wait_ge(tern_step, 2)
            nc.vector.tensor_scalar(wscale[:, 2:3], wscale[:, 1:2], -1.0, None, ALU.mult).then_inc(tern_step, 1)
            dve.wait_ge(tern_step, 3)
            nc.vector.tensor_scalar(below[:, :, :], w_ffn_sb[:, :, :], wscale[:, 2:3], None, ALU.is_lt
                                    ).then_inc(tern_step, 1)
            dve.wait_ge(bias_ready, 4)
            query_rest(0, 0)
            dve.wait_ge(tern_step, 4)
            nc.vector.scalar_tensor_tensor(out=tern[:, :, :], in0=w_ffn_sb[:, :, :], scalar=wscale[:, 1:2],
                                           in1=below[:, :, :], op0=ALU.is_gt, op1=ALU.subtract
                                           ).then_inc(tern_ready, 1)
            x_rest(1)
            query_rest(0, 1)
            sel_rest(1, 0)
            query_row_terms(0, range(NT))
            query_rest(0, 2)
            ln1_stats(X_BLK)
            query_rest(0, 3)
            dve.wait_ge(h_conv_ready, 2)
            ln1_stats(CONV_BLK)
            channel_shift(1, 1)
            channel_softmax(1, 1)
            dve.wait_ge(h_ext_ready, 3)
            ln1_stats(XEXT_BLK)
            value_rest(0, 0)
            sel_rest(1, 1)
            value_rest(0, 1)
            value_rest(0, 2)
            dve.wait_ge(h_ext_ready, 4)
            ln1_stats(CEXT_BLK)
            ln1_finish_stats(1)
            ln1_scale(1)
            value_rest(0, 3)
            embed(2)
            channel_shift(2, 0)

            def batch(b, prev, tower, embed_next):
                f, g = b + 1, b + 2
                if tower:
                    channel_softmax(g, 0)
                score_shift(b, 0)
                if tower:
                    x_rest(g)
                turn_p(b, 0)
                score_shift(b, 1)
                if tower:
                    sel_rest(g, 0)
                turn_p(b, 1)
                score_shift(b, 2)
                if prev:
                    for c in DVE_CHUNKS:
                        n2t_rest_moved(b - 1, c)
                score_shift(b, 3)
                turn_p(b, 2)
                turn_p(b, 3)
                if prev:
                    for c in DVE_CHUNKS:
                        nt_rest_moved(b, c)
                else:
                    for c in range(NT):
                        nt_rest(f, c, (fr + tp)[c])
                if tower:
                    channel_shift(g, 1)
                if prev:
                    add_ffn(b - 1, 0)
                    add_ffn(b - 1, 1)
                if tower:
                    channel_softmax(g, 1)
                    ln1_stats(X_BLK)
                    dve.wait_ge(h_conv_ready, g + 1)
                    ln1_stats(CONV_BLK)
                if prev:
                    add_ffn(b - 1, 2)
                if tower:
                    dve.wait_ge(h_ext_ready, 2 * g + 1)
                    ln1_stats(XEXT_BLK)
                if prev:
                    add_ffn(b - 1, 3)
                query_rest(f, 0)
                if tower:
                    sel_rest(g, 1)
                query_row_terms(f, range(NT))
                query_rest(f, 1)
                if tower:
                    dve.wait_ge(h_ext_ready, 2 * g + 2)
                    ln1_stats(CEXT_BLK)
                    ln1_finish_stats(g)
                pt_rest_moved(b, 2)
                pt_rest_moved(b, 3)
                if tower:
                    ln1_scale(g)
                query_rest(f, 2)
                if tower:
                    turn_n(g, 0)
                query_rest(f, 3)
                if tower:
                    turn_n(g, 1)
                add_attention(b, 0)
                ln2_stats(b, 0)
                if tower:
                    turn_n(g, 2)
                    turn_n(g, 3)
                for j in range(NT):
                    if j < NT - 1:
                        add_attention(b, j + 1)
                    ln2_scale(b, j)
                    if j < NT - 1:
                        ln2_stats(b, j + 1)
                    if j == NT - 1:
                        value_rest(f, 0)
                    turn_n2(b, j)
                value_rest(f, 1)
                value_rest(f, 2)
                if embed_next:
                    embed(g + 1)
                value_rest(f, 3)
                if embed_next:
                    channel_shift(g + 1, 0)

            batch(0, False, True, True)
            with dve.Fori(1, B - 3) as b:
                batch(b, True, True, True)
            batch(B - 3, True, True, False)
            batch(B - 2, True, False, False)

            last, before = B - 1, B - 2
            score_shift(last, 0)
            score_shift(last, 1)
            score_shift(last, 2)
            prob_rest(last, 0)
            score_shift(last, 3)
            prob_rest(last, 1)
            for c in DVE_CHUNKS:
                n2t_rest_moved(before, c)
            prob_rest(last, 2)
            prob_rest(last, 3)
            add_attention(last, 0)
            ln2_stats(last, 0)
            for j in range(NT):
                if j < NT - 1:
                    add_attention(last, j + 1)
                ln2_scale(last, j)
                if j < NT - 1:
                    ln2_stats(last, j + 1)
                if j > 0:
                    add_ffn(before, j - 1)
            n2_rest(last, 0)
            add_ffn(before, NT - 1)
            for j in range(1, NT):
                n2_rest(last, j)
                add_ffn(last, j - 1, h1_ffn_last, y_last)
            add_ffn(last, NT - 1, h1_ffn_last, y_last)


def position_table():
    import numpy as np
    depth = P // 2
    times = np.arange(T, dtype=np.float32)[:, None]
    depths = np.arange(depth, dtype=np.float32)[None, :] / np.float32(depth)
    rate = (np.float32(1.0) / np.power(np.float32(10000.0), depths)).astype(np.float32)
    angle = (times * rate).astype(np.float32)
    table = np.concatenate([np.sin(angle), np.cos(angle)], axis=-1).astype(np.float32)
    return np.ascontiguousarray(table.reshape(NT, P, P).transpose(1, 0, 2))


def kernel(x, L0_tok_emb_table, L0_tok_conv_w, L0_tok_conv_b, L0_tok_spos0, L0_tok_spos1, L0_attn_w_qkv,
           L0_attn_b_qkv, L0_attn_w_out, L0_attn_b_out, L0_ffn_weight, L0_ffn_bias):
    import numpy as np
    import concourse.bacc as bacc
    from concourse.bass_utils import run_bass_kernel_spmd

    B = x.shape[0]
    cols = [
        ("ids", np.asarray(x).reshape(B * NT, P).T),
        ("emb", L0_tok_emb_table),
        ("pos", position_table()),
        ("conv_w", np.asarray(L0_tok_conv_w).transpose(1, 2, 0)),
        ("conv_b", np.asarray(L0_tok_conv_b).reshape(P, 1)),
        ("spos0", L0_tok_spos0),
        ("spos1", L0_tok_spos1),
        ("w_qkv", L0_attn_w_qkv),
        ("b_qkv", np.asarray(L0_attn_b_qkv).reshape(3 * NT, P).T),
        ("w_out_t", np.asarray(L0_attn_w_out).T),
        ("b_out", L0_attn_b_out),
        ("w_ffn_t", np.asarray(L0_ffn_weight).T),
        ("b_ffn", L0_ffn_bias),
    ]
    nc = bacc.Bacc("TRN2", target_bir_lowering=False, num_devices=1)
    arrays, args = {}, []
    for name, a in cols:
        a = np.ascontiguousarray(a)
        arrays[f"in_{name}"] = a
        args.append(nc.dram_tensor(f"in_{name}", a.shape, mybir.dt.from_np(a.dtype), kind="ExternalInput").ap())
    args.append(nc.dram_tensor("out_h", (B, T, T), F32, kind="ExternalOutput").ap())
    lm_tower(nc, *args)
    r = run_bass_kernel_spmd(nc, [arrays], core_ids=[0])
    return r.results[0]["out_h"]
```

```python
from contextlib import ExitStack

import concourse.bass as bass
from concourse import mybir

ALU = mybir.AluOpType
ACT = mybir.ActivationFunctionType
F32 = mybir.dt.float32
F16 = mybir.dt.float16
I32 = mybir.dt.int32
U32 = mybir.dt.uint32
AX_X = mybir.AxisListType.X

P = 128
T = 512
NT = T // P
PAD = 2
BLK = 32
TAPS = 3
LN_EPS = 1e-5
W_EPS = 1e-10
W_UP = 64.0
SEL_UP = 1024.0
SCALE = float(T) ** -0.5

X_BLK, XEXT_BLK, CONV_BLK, CEXT_BLK = range(4)

SOFTPOS_STEPS = 5
LN1_STEPS = 11
LN2_STEPS = 5

SCORE_BANK = (0, 1, 2, 3)
FFN_BANK = (4, 5, 0, 1)
QUERY_BANK = (2, 3, 4, 5)
ATTEND_BANK = (0, 1, 2, 3)
VALUE_BANK = (4, 5, 0, 1)

POOL_CHUNKS = (0, 1)
DVE_CHUNKS = (2, 3)


def lm_tower(nc, ids, emb, pos, conv_w, conv_b, spos0, spos1, w_qkv, b_qkv, w_out_t, b_out, w_ffn_t, b_ffn, out):
    B = out.shape[0]
    ctx = ExitStack()
    with ctx:
        def sb(name, shape, dt=F32):
            return ctx.enter_context(nc.sbuf_tensor(name, shape, dt))

        def sem(name):
            return ctx.enter_context(nc.semaphore(name))

        ids_sb = sb("ids_sb", [P, B * NT], I32)
        ident = sb("ident", [P, P])
        ones = sb("ones", [P, P])
        pos_sb = sb("pos_sb", [P, NT, P])
        conv_w_sb = sb("conv_w_sb", [P, TAPS, P])
        conv_b_sb = sb("conv_b_sb", [P, 1])
        spos_sb = sb("spos_sb", [P, 2, P])
        conv_w_hi = sb("conv_w_hi", [P, TAPS, P], F16)
        conv_w_lo = sb("conv_w_lo", [P, TAPS, P], F16)
        spos_hi = sb("spos_hi", [P, 2, P], F16)
        spos_lo = sb("spos_lo", [P, 2, P], F16)
        w_sb = sb("w_sb", [P, 5 * NT, T])
        w_qkv_sb = w_sb[:, 0:3 * NT, :]
        b_qkv_sb = sb("b_qkv_sb", [P, 3 * NT])
        w_out_sb = w_sb[:, 3 * NT:4 * NT, :]
        w_ffn_sb = w_sb[:, 4 * NT:5 * NT, :]
        b_out_sb = sb("b_out_sb", [P, T])
        b_ffn_sb = sb("b_ffn_sb", [P, T])
        b_wide = sb("b_wide", [P, 2, NT, P])
        m_hi = sb("m_hi", [P, NT, T], F16)
        m_lo = sb("m_lo", [P, NT, T], F16)
        vo_hi = sb("vo_hi", [P, NT, T], F16)
        vo_lo = sb("vo_lo", [P, NT, T], F16)
        tern = sb("tern", [P, NT, T], F16)
        q_bias = sb("q_bias", [P, NT])
        key_row = sb("key_row", [P, T])
        bqbk = sb("bqbk", [P, 1])
        attn_bias = sb("attn_bias", [P, T])
        wsum = sb("wsum", [P, 1])
        wscale = sb("wscale", [P, 3])

        idx = sb("idx", [P, NT], I32)
        gathered_sb = sb("gathered_sb", [P, NT, P])
        xe = sb("xe", [P, NT, P])
        ch_max = sb("ch_max", [P, 2, NT])
        ch_sum = sb("ch_sum", [P, 2, NT])
        ch_rcp = sb("ch_rcp", [P, 2, NT])
        shifted = sb("shifted", [P, NT, P])
        ch_exp = sb("ch_exp", [P, NT, P])
        sel = sb("sel", [P, NT, P])
        x_hi = sb("x_hi", [P, PAD + T], F16)
        x_lo = sb("x_lo", [P, PAD + T], F16)
        sel_hi = sb("sel_hi", [P, T], F16)
        sel_lo = sb("sel_lo", [P, T], F16)
        h = sb("h", [P, NT, T])
        h_attn = sb("h_attn", [P, NT, T])
        stats1 = sb("stats1", [P, NT, 6])
        mv1 = sb("mv1", [P, NT, 2])
        rstd1 = sb("rstd1", [P, 5, NT])
        n = sb("n", [P, NT, T])
        junk = sb("junk", [P, T])
        row_term = sb("row_term", [P, NT])
        nt_hi = sb("nt_hi", [P, NT, T], F16)
        nt_lo = sb("nt_lo", [P, NT, T], F16)
        q_hi = sb("q_hi", [P, NT, T], F16)
        q_lo = sb("q_lo", [P, NT, T], F16)
        v_hi = sb("v_hi", [P, NT, T], F16)
        v_lo = sb("v_lo", [P, NT, T], F16)
        s_max = sb("s_max", [P, NT])
        s_top = sb("s_top", [P, NT])
        s_bias = sb("s_bias", [P, NT])
        prob = sb("prob", [P, NT, T])
        p_sum = sb("p_sum", [P, NT])
        p_rcp = sb("p_rcp", [P, NT])
        pt_hi = sb("pt_hi", [P, NT, T], F16)
        pt_lo = sb("pt_lo", [P, NT, T], F16)
        h1 = sb("h1", [P, NT, T])
        h1_ffn = sb("h1_ffn", [P, NT, T])
        stats2 = sb("stats2", [P, NT, 6])
        mv2 = sb("mv2", [P, NT, 2])
        rstd2 = sb("rstd2", [P, 5, NT])
        n2 = sb("n2", [P, NT, T])
        n2t_hi = sb("n2t_hi", [P, NT, T], F16)
        n2t_lo = sb("n2t_lo", [P, NT, T], F16)
        y = sb("y", [P, NT, T])
        below = y
        def wide_room(at):
            return w_sb[:, at:at + 6, :].rearrange("p c t -> p (c t)").rearrange("p (m x) -> p m x", m=NT)

        n_blocks, n_t = wide_room(0), wide_room(6)
        X_PART, SEL_PART = slice(T, T + P), slice(T + P, T + 2 * P)
        p_blocks = w_out_sb
        p_t = prob
        n2_blocks = w_ffn_sb
        n2_t = n2
        h1_ffn_last, y_last = h_attn, n
        ln_eps = sb("ln_eps", [P, 1])
        spare = sb("spare", [P, 1])

        mm = [ctx.enter_context(nc.psum_tensor(f"mm{k}", [P, T], F32)) for k in range(6)]
        tp = mm[4:6]
        fr = [ctx.enter_context(nc.psum_tensor(f"fr{k}", [P, T], F32)) for k in range(2)]

        ids_loaded = sem("ids_loaded")
        pos_loaded = sem("pos_loaded")
        tower_loaded = sem("tower_loaded")
        qk_loaded = [sem(f"qk_loaded{c}") for c in range(NT)]
        out_loaded = sem("out_loaded")
        ffn_loaded = sem("ffn_loaded")
        ident_zeroed = sem("ident_zeroed")
        consts_ready = sem("consts_ready")
        pads_zeroed = sem("pads_zeroed")
        wide_ready = sem("wide_ready")
        small_high = sem("small_high")
        small_split = sem("small_split")
        merged_ready = sem("merged_ready")
        merged_hi = sem("merged_hi")
        merged_split = sem("merged_split")
        bias_mm_ready = sem("bias_mm_ready")
        bias_ready = sem("bias_ready")
        abs_ready = sem("abs_ready")
        abs_total = sem("abs_total")
        tern_step = sem("tern_step")
        tern_ready = sem("tern_ready")
        idx_ready = sem("idx_ready")
        rows_gathered = sem("rows_gathered")
        xe_ready = sem("xe_ready")
        x_t_ready = sem("x_t_ready")
        h_x_ready = sem("h_x_ready")
        softpos_step = [sem(f"softpos_step{w}") for w in range(2)]
        ch_exp_ready = [sem(f"ch_exp_ready{w}") for w in range(2)]
        front_turned = sem("front_turned")
        sel_t_ready = sem("sel_t_ready")
        sel_high = sem("sel_high")
        sel_split = sem("sel_split")
        x_split = sem("x_split")
        conv_ready = sem("conv_ready")
        h_conv_ready = sem("h_conv_ready")
        conv_t_ready = sem("conv_t_ready")
        ext_ready = sem("ext_ready")
        h_ext_ready = sem("h_ext_ready")
        ln1_step = sem("ln1_step")
        ln1_root = sem("ln1_root")
        n_scale_ready = sem("n_scale_ready")
        n_ready = sem("n_ready")
        n_turned = sem("n_turned")
        n_moved = sem("n_moved")
        row_term_ready = sem("row_term_ready")
        h_attn_ready = sem("h_attn_ready")
        nt_ready, nt_high, nt_split = sem("nt_ready"), sem("nt_high"), sem("nt_split")
        q_ready, q_high, q_split = sem("q_ready"), sem("q_high"), sem("q_split")
        v_ready, v_high, v_split = sem("v_ready"), sem("v_high"), sem("v_split")
        scores_ready = sem("scores_ready")
        shift_step = sem("shift_step")
        prob_ready = sem("prob_ready")
        pt_ready, pt_high, pt_split = sem("pt_ready"), sem("pt_high"), sem("pt_split")
        p_turned = sem("p_turned")
        p_moved = sem("p_moved")
        h1_begun = sem("h1_begun")
        p_rcp_ready = sem("p_rcp_ready")
        o_ready = sem("o_ready")
        h1_ready = sem("h1_ready")
        h1_ffn_ready = sem("h1_ffn_ready")
        ln2_step = sem("ln2_step")
        ln2_root = sem("ln2_root")
        n2_scale_ready = sem("n2_scale_ready")
        n2_ready = sem("n2_ready")
        n2_turned = sem("n2_turned")
        n2_moved = sem("n2_moved")
        n2t_high = sem("n2t_high")
        n2t_low_pool = sem("n2t_low_pool")
        n2t_low_dve = sem("n2t_low_dve")
        n2t_ready, n2t_split = sem("n2t_ready"), sem("n2t_split")
        f_ready = sem("f_ready")
        y_ready = sem("y_ready")
        y_stored = sem("y_stored")

        def half(j):
            return slice(j * P, (j + 1) * P)

        def chunk(moved, c):
            return moved.rearrange("p i (c j b) -> p c j i b", c=NT, j=NT)[:, c, :, :, :]

        def front(part):
            return n_t[:, :, part].rearrange("p i (j b) -> p j i b", j=NT)

        def rows(tile):
            return tile.rearrange("p (j i b) -> p j i b", j=NT, i=NT)

        block = ctx.enter_context(nc.Block())

        @block.sync
        def _(sp):
            sp.sem_inc(y_stored, 64)
            sp.dma_start(ids_sb[:, :], ids).then_inc(ids_loaded, 16)

            def load_qk(c):
                for part in range(2):
                    sp.dma_start(w_qkv_sb[:, part * NT + c, :], w_qkv[part * T + c * P:part * T + (c + 1) * P, :]
                                 ).then_inc(qk_loaded[c], 16)

            load_qk(0)
            sp.dma_start(pos_sb[:, :, :], pos).then_inc(pos_loaded, 16)
            sp.dma_start(conv_w_sb[:, :, :], conv_w).then_inc(tower_loaded, 16)
            sp.dma_start(conv_b_sb[:, :], conv_b).then_inc(tower_loaded, 16)
            sp.dma_start(spos_sb[:, 0, :], spos0).then_inc(tower_loaded, 16)
            sp.dma_start(spos_sb[:, 1, :], spos1).then_inc(tower_loaded, 16)
            sp.dma_start(b_qkv_sb[:, :], b_qkv).then_inc(tower_loaded, 16)
            for c in range(1, NT):
                load_qk(c)
            sp.wait_ge(rows_gathered, 64)
            sp.dma_start(w_qkv_sb[:, 2 * NT:, :],
                         w_qkv[2 * T:, :].rearrange("(c p) t -> p c t", p=P)).then_inc(out_loaded, 16)
            sp.dma_start(w_out_sb[:, :, :], w_out_t.rearrange("(c p) t -> p c t", p=P)).then_inc(out_loaded, 16)
            sp.dma_start(b_out_sb[:, :], b_out.partition_broadcast(P)).then_inc(out_loaded, 16)
            sp.dma_start(w_ffn_sb[:, :, :], w_ffn_t.rearrange("(c p) t -> p c t", p=P)).then_inc(ffn_loaded, 16)
            sp.dma_start(b_ffn_sb[:, :], b_ffn.partition_broadcast(P)).then_inc(ffn_loaded, 16)

            def move_blocks(dst, src, turned, b, moved):
                sp.wait_ge(turned, 4 * b + 4)
                for i in range(NT):
                    for m in range(NT):
                        sp.dma_start(dst[m * BLK:(m + 1) * BLK, i, :], src[i * BLK:(i + 1) * BLK, m, :]
                                     ).then_inc(moved, 16)

            def store_rows(b):
                for j in range(NT):
                    sp.wait_ge(y_ready, 4 * b + (j + 5))
                    sp.dma_start(out[b, half(j), :], y[:, j, :]).then_inc(y_stored, 16)

            def batch(b, prev, tower, front_next):
                move_blocks(p_t, p_blocks, p_turned, b, p_moved)
                if prev:
                    store_rows(b - 1)
                if front_next:
                    sp.wait_ge(front_turned, 2 * b + 2)
                if tower:
                    move_blocks(n_t, n_blocks, n_turned, b, n_moved)
                move_blocks(n2_t, n2_blocks, n2_turned, b, n2_moved)

            batch(0, False, True, True)
            with sp.Fori(1, B - 3) as b:
                batch(b, True, True, True)
            batch(B - 3, True, True, False)
            batch(B - 2, True, False, False)
            store_rows(B - 2)
            for j in range(NT):
                sp.wait_ge(y_ready, 4 * (B - 1) + (j + 5))
                sp.dma_start(out[B - 1, half(j), :], y_last[:, j, :]).then_inc(y_stored, 16)
            sp.wait_ge(y_stored, 64 * (B + 1))

        @block.gpsimd
        def _(pool):
            nc.gpsimd.memset(ident[:, :], 0.0).then_inc(ident_zeroed, 1)
            nc.gpsimd.memset(x_hi[:, 0:PAD], 0.0).then_inc(pads_zeroed, 1)
            nc.gpsimd.memset(x_lo[:, 0:PAD], 0.0).then_inc(pads_zeroed, 1)
            nc.gpsimd.memset(ones[:, :], 1.0).then_inc(consts_ready, 1)
            nc.gpsimd.memset(ln_eps[:, :], LN_EPS).then_inc(consts_ready, 1)
            pool.wait_ge(ident_zeroed, 1)
            nc.gpsimd.affine_select(out=ident[:, :], in_=ident[:, :], compare_op=ALU.not_equal, fill=1.0,
                                    base=0, pattern=[[-1, P]], channel_multiplier=1).then_inc(consts_ready, 1)
            pool.wait_ge(ids_loaded, 16)

            def take_ids(b):
                nc.gpsimd.tensor_copy(idx[:, :], ids_sb[:, bass.ts(b, NT)]).then_inc(idx_ready, 1)

            def gather():
                for c in range(NT):
                    nc.gpsimd.indirect_dma_start(
                        out=gathered_sb[:, c, :], out_offset=None, in_=emb,
                        in_offset=bass.IndirectOffsetOnAxis(ap=idx[:, c:c + 1], axis=0)
                    ).then_inc(rows_gathered, 16)

            def add_attention_bias(j):
                nc.gpsimd.tensor_tensor(out=h_attn[:, j, :], in0=h[:, j, :], in1=attn_bias[:, :],
                                        op=ALU.add).then_inc(h_attn_ready, 1)

            def add_ffn_bias(b):
                pool.wait_ge(y_ready, 4 * b + 4)
                for j in range(NT):
                    pool.wait_ge(h1_ready, 4 * b + (j + 1))
                    nc.gpsimd.tensor_tensor(out=h1_ffn[:, j, :], in0=h1[:, j, :], in1=b_ffn_sb[:, :],
                                            op=ALU.add).then_inc(h1_ffn_ready, 1)

            take_ids(0)
            pool.wait_ge(idx_ready, 1)
            gather()
            pool.wait_ge(xe_ready, 1)
            pool.wait_ge(rows_gathered, 64)
            take_ids(1)
            pool.wait_ge(idx_ready, 2)
            gather()
            pool.wait_ge(xe_ready, 2)
            pool.wait_ge(rows_gathered, 128)
            take_ids(2)
            pool.wait_ge(idx_ready, 3)
            gather()
            pool.wait_ge(bias_ready, 4)
            pool.wait_ge(ffn_loaded, 32)
            pool.wait_ge(n_ready, 4)
            for j in range(NT):
                add_attention_bias(j)

            def low(dst, src, hi, high_done, at, done):
                pool.wait_ge(high_done, at)
                nc.gpsimd.tensor_tensor(out=rows(dst), in0=src, in1=rows(hi), op=ALU.subtract).then_inc(done, 1)

            def batch(b, prev, gather_next):
                pool.wait_ge(n_ready, 4 * b + 8)
                for j in range(NT - 1):
                    pool.wait_ge(h1_begun, 4 * b + (j + 1))
                    add_attention_bias(j)
                e = b + (4 if prev else 3)
                if gather_next:
                    pool.wait_ge(xe_ready, e)
                    take_ids(e)
                    pool.wait_ge(idx_ready, e + 1)
                pool.wait_ge(h1_begun, 4 * b + 4)
                add_attention_bias(NT - 1)
                if prev:
                    for c in POOL_CHUNKS:
                        low(n2t_lo[:, c, :], chunk(n2_t, c), n2t_hi[:, c, :], n2t_high, 4 * b + (c - 3), n2t_low_pool)
                    for c in POOL_CHUNKS:
                        low(nt_lo[:, c, :], chunk(n_t[:, :, 0:T], c), nt_hi[:, c, :], nt_high, 4 * b + (c + 5),
                            nt_split)
                if gather_next:
                    gather()
                for c in range(NT - 1):
                    low(pt_lo[:, c, :], chunk(p_t, c), pt_hi[:, c, :], pt_high, 4 * b + (c + 1), pt_split)
                if not prev:
                    pool.wait_ge(xe_ready, 4)
                    take_ids(4)
                    pool.wait_ge(idx_ready, 5)
                    gather()
                add_ffn_bias(b)

            batch(0, False, True)
            with pool.Fori(1, B - 4) as b:
                batch(b, True, True)
            batch(B - 4, True, False)
            batch(B - 3, True, False)
            batch(B - 2, True, False)
            for c in POOL_CHUNKS:
                low(n2t_lo[:, c, :], chunk(n2_t, c), n2t_hi[:, c, :], n2t_high, 4 * (B - 2) + (c + 1), n2t_low_pool)
            for j in range(NT):
                pool.wait_ge(h1_ready, 4 * (B - 1) + (j + 1))
                nc.gpsimd.tensor_tensor(out=h1_ffn_last[:, j, :], in0=h1[:, j, :], in1=b_ffn_sb[:, :],
                                        op=ALU.add).then_inc(h1_ffn_ready, 1)

        @block.tensor
        def _(pe):
            def transpose4(dst, src, done):
                for c in range(NT):
                    last = nc.tensor.transpose(dst[:, half(c)], src(c), ident[:, :])
                last.then_inc(done, 1)

            def split_product(dst, a_hi, a_lo, b_hi, b_lo, done):
                for c in range(NT):
                    nc.tensor.matmul(dst[:, :], a_hi(c), b_hi(c), start=(c == 0), stop=False)
                    nc.tensor.matmul(dst[:, :], a_hi(c), b_lo(c), start=False, stop=False)
                    last = nc.tensor.matmul(dst[:, :], a_lo(c), b_hi(c), start=False, stop=(c == NT - 1))
                last.then_inc(done, 1)

            def x_transpose(f):
                pe.wait_ge(xe_ready, f + 1)
                transpose4(fr[0], lambda c: xe[:, c, :], x_t_ready)

            def sel_transpose(f, w):
                pe.wait_ge(softpos_step[w], SOFTPOS_STEPS * (f + 1))
                transpose4(fr[1], lambda c: sel[:, c, :], sel_t_ready)

            def convolution(f):
                pe.wait_ge(x_split, f + 1)
                for k in range(TAPS):
                    nc.tensor.matmul(fr[0][:, :], conv_w_hi[:, k, :], x_hi[:, k:k + T], start=(k == 0), stop=False)
                    nc.tensor.matmul(fr[0][:, :], conv_w_hi[:, k, :], x_lo[:, k:k + T], start=False, stop=False)
                    last = nc.tensor.matmul(fr[0][:, :], conv_w_lo[:, k, :], x_hi[:, k:k + T],
                                            start=False, stop=(k == TAPS - 1))
                last.then_inc(conv_ready, 1)

            def conv_transpose(f):
                pe.wait_ge(h_conv_ready, f + 1)
                transpose4(fr[1], lambda c: h[:, CONV_BLK, half(c)], conv_t_ready)

            def extension(f, w):
                pe.wait_ge(sel_split, 2 * f + (w + 1))
                if w == 0:
                    pe.wait_ge(h_conv_ready, f + 1)
                else:
                    pe.wait_ge(h_ext_ready, 2 * f + 1)
                nc.tensor.matmul(fr[0][:, :], spos_hi[:, w, :], sel_hi[:, :], start=True, stop=False)
                nc.tensor.matmul(fr[0][:, :], spos_hi[:, w, :], sel_lo[:, :], start=False, stop=False)
                nc.tensor.matmul(fr[0][:, :], spos_lo[:, w, :], sel_hi[:, :], start=False, stop=True
                                 ).then_inc(ext_ready, 1)

            def nt_transpose(f, j, bank):
                pe.wait_ge(n_ready, 4 * f + 4)
                transpose4(bank, lambda c: n[:, c, half(j)], nt_ready)

            def queries(b, j):
                pe.wait_ge(nt_split, 4 * b + 4)
                split_product(mm[QUERY_BANK[j]], lambda c: m_hi[:, c, half(j)], lambda c: m_lo[:, c, half(j)],
                              lambda c: nt_hi[:, c, :], lambda c: nt_lo[:, c, :], q_ready)

            def values(b, j):
                split_product(mm[VALUE_BANK[j]], lambda c: nt_hi[:, c, half(j)], lambda c: nt_lo[:, c, half(j)],
                              lambda c: vo_hi[:, c, :], lambda c: vo_lo[:, c, :], v_ready)

            def scores(b, j):
                if j < 2:
                    pe.wait_ge(v_split, 4 * b + (j + 3))
                if j == 0:
                    pe.wait_ge(q_split, 4 * b + 4)
                split_product(mm[SCORE_BANK[j]], lambda c: q_hi[:, c, half(j)], lambda c: q_lo[:, c, half(j)],
                              lambda c: nt_hi[:, c, :], lambda c: nt_lo[:, c, :], scores_ready)

            def prob_transpose(b, j):
                pe.wait_ge(prob_ready, 4 * b + (j + 1))
                if j >= 2:
                    pe.wait_ge(pt_split, 4 * b + (j - 1))
                transpose4(fr[j % 2], lambda c: prob[:, j, half(c)], pt_ready)

            def attend(b, j, split):
                pe.wait_ge(pt_split, split)
                split_product(mm[ATTEND_BANK[j]], lambda c: pt_hi[:, c, half(j)], lambda c: pt_lo[:, c, half(j)],
                              lambda c: v_hi[:, c, :], lambda c: v_lo[:, c, :], o_ready)

            def n2_transpose(b, j):
                pe.wait_ge(n2_ready, 4 * b + (j + 1))
                if j >= 2:
                    pe.wait_ge(n2t_split, j - 1)
                transpose4(fr[j % 2], lambda c: n2[:, j, half(c)], n2t_ready)

            def ffn(j, chunk_waits):
                bank = FFN_BANK[j]
                for at, (c, half_done, count) in enumerate(chunk_waits):
                    if half_done is not None:
                        pe.wait_ge(half_done, count)
                    nc.tensor.matmul(mm[bank][:, :], n2t_hi[:, c, half(j)], tern[:, c, :],
                                     start=(at == 0), stop=False)
                    last = nc.tensor.matmul(mm[bank][:, :], n2t_lo[:, c, half(j)], tern[:, c, :],
                                            start=False, stop=(at == NT - 1))
                last.then_inc(f_ready, 1)

            def ffn_moved(b, j):
                order = ((0, n2t_low_pool, 2 * b + 1), (2, n2t_low_dve, 2 * b + 1),
                         (3, n2t_low_dve, 2 * b + 2), (1, n2t_low_pool, 2 * b + 2))
                ffn(j, [(c, half_done if j == 0 else None, count) for c, half_done, count in order])

            def ffn_last(j):
                ffn(j, [(c, n2t_split if c == 0 else None, j + 1) for c in range(NT)])

            def key_query_merge(c):
                pe.wait_ge(qk_loaded[c], 32)
                for j in range(NT):
                    step = nc.tensor.matmul(mm[j][:, :], w_qkv_sb[:, c, half(j)], w_qkv_sb[:, NT + c, :],
                                            start=(c == 0), stop=(c == NT - 1))
                    if c == NT - 1:
                        step.then_inc(merged_ready, 1)

            def value_out_merge(j):
                pe.wait_ge(merged_split, j + 1)
                for c in range(NT):
                    last = nc.tensor.matmul(mm[j][:, :], w_qkv_sb[:, 2 * NT + c, half(j)], w_out_sb[:, c, :],
                                            start=(c == 0), stop=(c == NT - 1))
                last.then_inc(merged_ready, 1)

            key_query_merge(0)
            pe.wait_ge(consts_ready, 3)
            pe.wait_ge(pads_zeroed, 2)
            key_query_merge(1)
            x_transpose(0)
            key_query_merge(2)
            sel_transpose(0, 0)
            pe.wait_ge(small_split, 2)
            convolution(0)
            key_query_merge(3)
            extension(0, 0)
            conv_transpose(0)
            pe.wait_ge(out_loaded, 48)
            value_out_merge(0)
            pe.wait_ge(wide_ready, 8)
            for j in range(NT):
                for c in range(NT):
                    nc.tensor.matmul(tp[0][:, j:j + 1], w_qkv_sb[:, NT + c, half(j)], b_qkv_sb[:, c:c + 1],
                                     start=(c == 0), stop=(c == NT - 1))
            for c in range(NT):
                last = nc.tensor.matmul(tp[0][:, NT:NT + 1], b_wide[:, 0, c, :], b_qkv_sb[:, c:c + 1],
                                        start=(c == 0), stop=(c == NT - 1))
            last.then_inc(bias_mm_ready, 1)
            sel_transpose(0, 1)
            value_out_merge(1)
            extension(0, 1)
            value_out_merge(2)
            for c in range(NT):
                last = nc.tensor.matmul(tp[1][:, :], b_wide[:, 0, c, :], w_qkv_sb[:, c, :],
                                        start=(c == 0), stop=(c == NT - 1))
            last.then_inc(bias_mm_ready, 1)
            pe.wait_ge(h_ext_ready, 2)
            nt_transpose(0, 0, fr[0])
            nt_transpose(0, 1, fr[1])
            value_out_merge(3)
            pe.wait_ge(nt_split, 2)
            nt_transpose(0, 2, fr[0])
            nt_transpose(0, 3, fr[1])
            pe.wait_ge(bias_ready, 3)
            for c in range(NT):
                last = nc.tensor.matmul(tp[0][:, :], b_wide[:, 1, c, :], w_out_sb[:, c, :],
                                        start=(c == 0), stop=(c == NT - 1))
            last.then_inc(bias_mm_ready, 1)
            pe.wait_ge(abs_ready, 1)
            nc.tensor.matmul(tp[1][:, 0:1], ones[:, :], wsum[:, :], start=True, stop=True).then_inc(abs_total, 1)
            pe.wait_ge(merged_split, 2 * NT)
            queries(0, 0)
            x_transpose(1)
            queries(0, 1)
            sel_transpose(1, 0)
            pe.wait_ge(bias_ready, 4)
            queries(0, 2)
            convolution(1)
            pe.wait_ge(tern_step, 1)
            queries(0, 3)
            extension(1, 0)
            conv_transpose(1)
            pe.wait_ge(q_split, 3)
            values(0, 0)
            pe.wait_ge(q_split, 4)
            values(0, 1)
            sel_transpose(1, 1)
            values(0, 2)
            extension(1, 1)
            values(0, 3)
            pe.wait_ge(tern_ready, 1)

            def batch(b, prev, tower):
                f, g = b + 1, b + 2
                scores(b, 0)
                if not prev:
                    pe.wait_ge(h_ext_ready, 2 * g)
                    x_transpose(g)
                scores(b, 1)
                if not prev:
                    sel_transpose(g, 0)
                scores(b, 2)
                scores(b, 3)
                if not prev:
                    pe.wait_ge(x_split, g + 1)
                    pe.wait_ge(sel_split, 2 * g + 1)
                    for j in range(NT):
                        nt_transpose(f, j, (fr + tp)[j])
                    pe.wait_ge(nt_split, 4 * f + 2)
                if tower and prev:
                    pe.wait_ge(h_ext_ready, 2 * g)
                if tower:
                    convolution(g)
                if prev:
                    ffn_moved(b - 1, 0)
                    ffn_moved(b - 1, 1)
                if tower and prev:
                    extension(g, 0)
                    conv_transpose(g)
                if prev:
                    pe.wait_ge(prob_ready, 4 * b + 1)
                    ffn_moved(b - 1, 2)
                if prev:
                    pe.wait_ge(prob_ready, 4 * b + 2)
                    ffn_moved(b - 1, 3)
                pe.wait_ge(prob_ready, 4 * b + 3)
                queries(f, 0)
                if not prev:
                    extension(g, 0)
                    conv_transpose(g)
                if tower and prev:
                    sel_transpose(g, 1)
                pe.wait_ge(prob_ready, 4 * b + 4)
                queries(f, 1)
                if not prev:
                    sel_transpose(g, 1)
                if tower and prev:
                    extension(g, 1)
                if prev:
                    pe.wait_ge(y_ready, 4 * b + 1)
                queries(f, 2)
                if not prev:
                    extension(g, 1)
                if prev:
                    pe.wait_ge(y_ready, 4 * b + 2)
                queries(f, 3)
                if prev:
                    pe.wait_ge(y_ready, 4 * b + 3)
                attend(b, 0, 4 * b + 4)
                if prev:
                    pe.wait_ge(y_ready, 4 * b + 4)
                attend(b, 1, 4 * b + 4)
                pe.wait_ge(q_split, 4 * f + 1)
                attend(b, 2, 4 * b + 4)
                pe.wait_ge(q_split, 4 * f + 2)
                attend(b, 3, 4 * b + 4)
                pe.wait_ge(q_split, 4 * f + 3)
                values(f, 0)
                pe.wait_ge(q_split, 4 * f + 4)
                values(f, 1)
                pe.wait_ge(h1_ready, 4 * b + 1)
                values(f, 2)
                pe.wait_ge(h1_ready, 4 * b + 2)
                values(f, 3)

            batch(0, False, True)
            with pe.Fori(1, B - 2) as b:
                batch(b, True, True)
            batch(B - 2, True, False)

            last, before = B - 1, B - 2
            scores(last, 0)
            scores(last, 1)
            scores(last, 2)
            prob_transpose(last, 0)
            scores(last, 3)
            prob_transpose(last, 1)
            attend(last, 0, 4 * last + 1)
            prob_transpose(last, 2)
            attend(last, 1, 4 * last + 2)
            prob_transpose(last, 3)
            attend(last, 2, 4 * last + 3)
            attend(last, 3, 4 * last + 4)
            ffn_moved(before, 0)
            ffn_moved(before, 1)
            n2_transpose(last, 0)
            pe.wait_ge(h1_ready, 4 * last + 1)
            ffn_moved(before, 2)
            n2_transpose(last, 1)
            pe.wait_ge(h1_ready, 4 * last + 2)
            ffn_moved(before, 3)
            for j in range(NT):
                if j < 2:
                    n2_transpose(last, j + 2)
                pe.wait_ge(y_ready, 4 * before + (j + 5))
                ffn_last(j)

        @block.scalar
        def _(act):
            def high(dst, src, ready, ready_at, done, bias=None):
                act.wait_ge(ready, ready_at)
                if bias is None:
                    nc.scalar.activation(dst, src, ACT.Copy).then_inc(done, 1)
                else:
                    nc.scalar.activation(dst, src, ACT.Identity, bias=bias).then_inc(done, 1)

            def channel_exp(f, w):
                act.wait_ge(softpos_step[w], SOFTPOS_STEPS * f + 2)
                nc.scalar.activation(ch_exp[:, :, :], shifted[:, :, :], ACT.Exp).then_inc(ch_exp_ready[w], 1)

            def store_x(f):
                act.wait_ge(x_t_ready, f + 1)
                nc.scalar.activation(x_hi[:, PAD:], fr[0][:, :], ACT.Copy)
                if not (isinstance(f, int) and f == 0):
                    act.wait_ge(h_attn_ready, 4 * f - 3)
                nc.scalar.activation(h[:, X_BLK, :], fr[0][:, :], ACT.Copy).then_inc(h_x_ready, 1)

            def sel_half(f, w):
                act.wait_ge(sel_t_ready, 2 * f + (w + 1) if isinstance(f, int) and f < 2 or w == 0 else f + 4)
                nc.scalar.activation(sel_hi[:, :], fr[1][:, :], ACT.Copy).then_inc(sel_high, 1)

            def store_x_moved(b):
                act.wait_ge(n_moved, 256 * b)
                nc.scalar.activation(rows(x_hi[:, PAD:]), front(X_PART), ACT.Copy)
                act.wait_ge(h_attn_ready, 4 * b + 5)
                nc.scalar.activation(rows(h[:, X_BLK, :]), front(X_PART), ACT.Copy).then_inc(h_x_ready, 1)

            def sel_half_moved(b):
                nc.scalar.activation(rows(sel_hi[:, :]), front(SEL_PART), ACT.Copy).then_inc(sel_high, 1)

            def store_conv(f):
                act.wait_ge(conv_ready, f + 1)
                if not (isinstance(f, int) and f == 0):
                    act.wait_ge(h_attn_ready, 4 * f)
                nc.scalar.activation(h[:, CONV_BLK, :], fr[0][:, :], ACT.Identity, bias=conv_b_sb[:, :],
                                     scale=1.0 / W_UP).then_inc(h_conv_ready, 1)

            def store_ext(f, w):
                act.wait_ge(ext_ready, 2 * f + (w + 1))
                blk = XEXT_BLK if w == 0 else CEXT_BLK
                nc.scalar.activation(h[:, blk, :], fr[0][:, :], ACT.Copy, scale=1.0 / (W_UP * SEL_UP)
                                     ).then_inc(h_ext_ready, 1)

            def rsqrt_guess(out_ln, out_rs, var, ready, ready_at, done, done_at):
                act.wait_ge(ready, ready_at)
                nc.scalar.activation(out_ln, var, ACT.Ln, bias=ln_eps[:, :]).then_inc(done, 1)
                act.wait_ge(done, done_at)
                nc.scalar.activation(out_rs, out_ln, ACT.Exp, scale=-0.5).then_inc(done, 1)

            def ln1_guess(f):
                rsqrt_guess(rstd1[:, 0, :], rstd1[:, 1, :], mv1[:, :, 1], ln1_step, LN1_STEPS * f + 8,
                            ln1_root, 2 * f + 1)

            def ln2_guess(b, j):
                rsqrt_guess(rstd2[:, 0, j:j + 1], rstd2[:, 1, j:j + 1], mv2[:, j, 1:2],
                            ln2_step, LN2_STEPS * (4 * b + j) + 2, ln2_root, 2 * (4 * b + j) + 1)

            def nt_half(f, j, bank):
                high(nt_hi[:, j, :], bank[:, :], nt_ready, 4 * f + (j + 1), nt_high)

            def ln1_normalise(f, blocks):
                act.wait_ge(n_scale_ready, f + 1)
                for j in blocks:
                    nc.scalar.activation(n[:, j, :], h[:, j, :], ACT.Identity, bias=rstd1[:, 4, j:j + 1],
                                         scale=rstd1[:, 3, j:j + 1]).then_inc(n_ready, 1)

            def ln2_normalise(b, j):
                act.wait_ge(n2_scale_ready, 4 * b + (j + 1))
                nc.scalar.activation(n2[:, j, :], h1[:, j, :], ACT.Identity, bias=rstd2[:, 4, j:j + 1],
                                     scale=rstd2[:, 3, j:j + 1]).then_inc(n2_ready, 1)

            def nt_half_moved(b, c):
                high(rows(nt_hi[:, c, :]), chunk(n_t[:, :, 0:T], c), n_moved, 256 * b, nt_high)

            def pt_half_moved(b, c):
                high(rows(pt_hi[:, c, :]), chunk(p_t, c), p_moved, 256 * b + 256, pt_high)

            def n2t_half_moved(b, c):
                high(rows(n2t_hi[:, c, :]), chunk(n2_t, c), n2_moved, 256 * b + 256, n2t_high)

            def query_half(b, j):
                high(q_hi[:, j, :], mm[QUERY_BANK[j]][:, :], q_ready, 4 * b + (j + 1), q_high,
                     bias=q_bias[:, j:j + 1])

            def value_half(b, j):
                high(v_hi[:, j, :], mm[VALUE_BANK[j]][:, :], v_ready, 4 * b + (j + 1), v_high)

            def score_exp(b, j):
                act.wait_ge(shift_step, 3 * (4 * b + j) + 3)
                nc.scalar.activation(prob[:, j, :], mm[SCORE_BANK[j]][:, :], ACT.Exp, bias=s_bias[:, j:j + 1],
                                     scale=SCALE, accum_out=p_sum[:, j:j + 1]).then_inc(prob_ready, 1)

            def prob_half(b, j):
                high(pt_hi[:, :, half(j)], fr[j % 2][:, :].rearrange("p (c k) -> p c k", c=NT),
                     pt_ready, j + 1, pt_high)

            def n2_half(b, j):
                act.wait_ge(f_ready, 4 * b + (j - 3))
                high(n2t_hi[:, :, half(j)], fr[j % 2][:, :].rearrange("p (c k) -> p c k", c=NT),
                     n2t_ready, j + 1, n2t_high)

            act.wait_ge(consts_ready, 3)
            nc.scalar.preload_act_table_set("natural_log_exp_and_others")
            act.wait_ge(tower_loaded, 80)
            nc.scalar.activation(conv_w_hi[:, :, :], conv_w_sb[:, :, :], ACT.Copy, scale=W_UP
                                 ).then_inc(small_high, 1)
            nc.scalar.activation(spos_hi[:, :, :], spos_sb[:, :, :], ACT.Copy, scale=W_UP).then_inc(small_high, 1)

            def merged_half(dst, j, at):
                high(dst[:, j, :], mm[j][:, :], merged_ready, at + j + 1, merged_hi)

            channel_exp(0, 0)
            store_x(0)
            sel_half(0, 0)
            store_conv(0)
            for j in range(NT):
                merged_half(m_hi, j, 0)
            store_ext(0, 0)
            channel_exp(0, 1)
            merged_half(vo_hi, 0, NT)
            sel_half(0, 1)
            merged_half(vo_hi, 1, NT)
            store_ext(0, 1)
            ln1_guess(0)
            ln1_normalise(0, range(NT))
            merged_half(vo_hi, 2, NT)
            nt_half(0, 0, fr[0])
            nt_half(0, 1, fr[1])
            merged_half(vo_hi, 3, NT)
            nt_half(0, 2, fr[0])
            nt_half(0, 3, fr[1])
            channel_exp(1, 0)
            act.wait_ge(bias_ready, 2)
            query_half(0, 0)
            store_x(1)
            query_half(0, 1)
            sel_half(1, 0)
            query_half(0, 2)
            store_conv(1)
            query_half(0, 3)
            store_ext(1, 0)
            channel_exp(1, 1)
            value_half(0, 0)
            sel_half(1, 1)
            value_half(0, 1)
            value_half(0, 2)
            store_ext(1, 1)
            ln1_guess(1)
            value_half(0, 3)
            ln1_normalise(1, range(NT))
            channel_exp(2, 0)

            def begin_h1(b):
                act.wait_ge(h_attn_ready, 4 * b + 4)
                for j in range(NT):
                    nc.scalar.activation(h1[:, j, :], h_attn[:, j, :], ACT.Copy).then_inc(h1_begun, 1)

            def batch(b, prev, tower, front_next, embed_next):
                f, g, e = b + 1, b + 2, b + 3
                if prev:
                    act.wait_ge(h1_ffn_ready, 4 * b)
                    act.wait_ge(n2_ready, 4 * b)
                begin_h1(b)
                if tower and prev:
                    store_x_moved(b)
                    sel_half_moved(b)
                elif tower:
                    store_x(g)
                score_exp(b, 0)
                if front_next and prev:
                    channel_exp(e, 0)
                if not prev:
                    sel_half(g, 0)
                score_exp(b, 1)
                if prev:
                    for c in range(NT):
                        n2t_half_moved(b - 1, c)
                score_exp(b, 2)
                score_exp(b, 3)
                if tower and prev:
                    store_conv(g)
                for c in range(NT):
                    if prev:
                        nt_half_moved(b, c)
                    else:
                        nt_half(f, c, (fr + tp)[c])
                if not prev:
                    channel_exp(e, 0)
                    store_conv(g)
                if tower:
                    store_ext(g, 0)
                    channel_exp(g, 1)
                query_half(f, 0)
                if tower:
                    sel_half(g, 1)
                query_half(f, 1)
                if tower:
                    store_ext(g, 1)
                for c in range(NT):
                    pt_half_moved(b, c)
                if tower:
                    ln1_guess(g)
                query_half(f, 2)
                if tower:
                    ln1_normalise(g, (0,))
                query_half(f, 3)
                if tower:
                    ln1_normalise(g, (1, 2, 3))
                ln2_guess(b, 0)
                ln2_normalise(b, 0)
                ln2_guess(b, 1)
                ln2_normalise(b, 1)
                ln2_guess(b, 2)
                ln2_normalise(b, 2)
                ln2_guess(b, 3)
                value_half(f, 0)
                ln2_normalise(b, 3)
                value_half(f, 1)
                value_half(f, 2)
                value_half(f, 3)

            batch(0, False, True, True, True)
            with act.Fori(1, B - 4) as b:
                batch(b, True, True, True, True)
            batch(B - 4, True, True, True, False)
            batch(B - 3, True, True, False, False)
            batch(B - 2, True, False, False, False)

            last, before = B - 1, B - 2
            act.wait_ge(h1_ffn_ready, 4 * last)
            act.wait_ge(n2_ready, 4 * last)
            begin_h1(last)
            score_exp(last, 0)
            score_exp(last, 1)
            score_exp(last, 2)
            prob_half(last, 0)
            score_exp(last, 3)
            prob_half(last, 1)
            for c in range(NT):
                n2t_half_moved(before, c)
            prob_half(last, 2)
            prob_half(last, 3)
            ln2_guess(last, 0)
            act.wait_ge(n2t_low_pool, 2 * last)
            act.wait_ge(n2t_low_dve, 2 * last)
            ln2_normalise(last, 0)
            ln2_guess(last, 1)
            ln2_normalise(last, 1)
            ln2_guess(last, 2)
            ln2_normalise(last, 2)
            n2_half(last, 0)
            ln2_guess(last, 3)
            ln2_normalise(last, 3)
            for j in range(1, NT):
                n2_half(last, j)

        @block.vector
        def _(dve):
            def low(dst, src, hi, high_done, at, done, bias=None):
                dve.wait_ge(high_done, at)
                if bias is None:
                    nc.vector.tensor_tensor(out=dst, in0=src, in1=hi, op=ALU.subtract).then_inc(done, 1)
                else:
                    nc.vector.scalar_tensor_tensor(out=dst, in0=src, scalar=bias, in1=hi, op0=ALU.add,
                                                   op1=ALU.subtract).then_inc(done, 1)

            def embed(f):
                dve.wait_ge(rows_gathered, 64 * (f + 1))
                if isinstance(f, int) and f == 0:
                    dve.wait_ge(pos_loaded, 16)
                if not (isinstance(f, int) and f < 4):
                    dve.wait_ge(front_turned, 2 * f - 6)
                nc.vector.scalar_tensor_tensor(out=xe[:, :, :], in0=gathered_sb[:, :, :], scalar=float(P) ** 0.5,
                                               in1=pos_sb[:, :, :], op0=ALU.mult, op1=ALU.add).then_inc(xe_ready, 1)

            def channel_shift(f, w):
                at = SOFTPOS_STEPS * f
                if w == 0:
                    dve.wait_ge(xe_ready, f + 1)
                    src = xe[:, :, :]
                else:
                    dve.wait_ge(conv_t_ready, f + 1)
                    src = fr[1][:, :].rearrange("p (c k) -> p c k", c=NT)
                nc.vector.reduce_max(ch_max[:, w, :], src, AX_X).then_inc(softpos_step[w], 1)
                dve.wait_ge(softpos_step[w], at + 1)
                nc.vector.tensor_tensor(out=shifted[:, :, :], in0=src,
                                        in1=ch_max[:, w, :].unsqueeze(2).to_broadcast([P, NT, P]),
                                        op=ALU.subtract).then_inc(softpos_step[w], 1)

            def channel_softmax(f, w):
                at = SOFTPOS_STEPS * f
                dve.wait_ge(ch_exp_ready[w], f + 1)
                nc.vector.reduce_sum(ch_sum[:, w, :], ch_exp[:, :, :], AX_X).then_inc(softpos_step[w], 1)
                dve.wait_ge(softpos_step[w], at + 3)
                nc.vector.reciprocal(ch_rcp[:, w, :], ch_sum[:, w, :]).then_inc(softpos_step[w], 1)
                dve.wait_ge(softpos_step[w], at + 4)
                if w == 1 and not (isinstance(f, int) and f < 2):
                    last = isinstance(f, int) and f == B - 1
                    dve.wait_ge(front_turned, 2 * f - (4 if last else 2))
                nc.vector.scalar_tensor_tensor(out=sel[:, :, :], in0=ch_exp[:, :, :], scalar=SEL_UP,
                                               in1=ch_rcp[:, w, :].unsqueeze(2).to_broadcast([P, NT, P]),
                                               op0=ALU.mult, op1=ALU.mult).then_inc(softpos_step[w], 1)

            def x_rest(f):
                low(x_lo[:, PAD:], fr[0][:, :], x_hi[:, PAD:], h_x_ready, f + 1, x_split)

            def sel_rest(f, w):
                dve.wait_ge(sel_high, 2 * f + (w + 1))
                nc.vector.tensor_tensor(out=sel_lo[:, :], in0=fr[1][:, :], in1=sel_hi[:, :],
                                        op=ALU.subtract).then_inc(sel_split, 1)

            def x_rest_moved(b):
                low(rows(x_lo[:, PAD:]), front(X_PART), rows(x_hi[:, PAD:]), h_x_ready, b + 3, x_split)

            def sel_rest_moved(b):
                dve.wait_ge(sel_high, 2 * b + 5)
                nc.vector.tensor_tensor(out=rows(sel_lo[:, :]), in0=front(SEL_PART), in1=rows(sel_hi[:, :]),
                                        op=ALU.subtract).then_inc(sel_split, 1)

            def turn_front(f):
                for tile, part, ready, at in ((xe, X_PART, xe_ready, f + 1),
                                              (sel, SEL_PART, softpos_step[0], SOFTPOS_STEPS * (f + 1))):
                    dve.wait_ge(ready, at)
                    nc.vector.transpose(n_blocks[:, :, part].rearrange("p m (j b) -> p j m b", j=NT).bitcast(U32),
                                        tile[:, :, :].rearrange("p j (m a) -> p j m a", m=NT).bitcast(U32)
                                        ).then_inc(front_turned, 1)

            def ln1_stats(blk):
                nc.vector.bn_stats(stats1[:, blk, :], h[:, blk, :]).then_inc(ln1_step, 1)

            def ln1_finish_stats(f):
                dve.wait_ge(ln1_step, LN1_STEPS * f + 4)
                nc.vector.memset(spare[:, :], 0.0)
                for j in range(NT):
                    nc.vector.bn_aggr(mv1[:, j, :], stats1[:, j, :]).then_inc(ln1_step, 1)

            def refine(r, var, root, root_at, step, at):
                dve.wait_ge(root, root_at)
                nc.vector.scalar_tensor_tensor(out=r[2], in0=var, scalar=LN_EPS, in1=r[1], op0=ALU.add,
                                               op1=ALU.mult).then_inc(step, 1)
                dve.wait_ge(step, at + 1)
                nc.vector.scalar_tensor_tensor(out=r[2], in0=r[2], scalar=-0.5, in1=r[1], op0=ALU.mult,
                                               op1=ALU.mult).then_inc(step, 1)
                dve.wait_ge(step, at + 2)
                return nc.vector.scalar_tensor_tensor(out=r[3], in0=r[2], scalar=1.5, in1=r[1], op0=ALU.add,
                                                      op1=ALU.mult)

            def ln1_scale(f):
                at = LN1_STEPS * f
                dve.wait_ge(ln1_step, at + 8)
                refine([rstd1[:, k, :] for k in range(4)], mv1[:, :, 1], ln1_root, 2 * f + 2, ln1_step, at + 8
                       ).then_inc(ln1_step, 1)
                dve.wait_ge(ln1_step, at + 11)
                nc.vector.scalar_tensor_tensor(out=rstd1[:, 4, :], in0=mv1[:, :, 0], scalar=-1.0,
                                               in1=rstd1[:, 3, :], op0=ALU.mult, op1=ALU.mult
                                               ).then_inc(n_scale_ready, 1)

            def query_row_terms(b, tiles):
                for j in tiles:
                    if j == 0:
                        dve.wait_ge(n_ready, 4 * b + 4)
                    else:
                        dve.wait_ge(row_term_ready, 4 * b + j)
                    nc.vector.tensor_tensor_reduce(out=junk[:, :], in0=n[:, j, :], in1=key_row[:, :], scale=1.0,
                                                   scalar=bqbk[:, :], op0=ALU.mult, op1=ALU.add,
                                                   accum_out=row_term[:, j:j + 1]).then_inc(row_term_ready, 1)

            def nt_rest(f, j, bank):
                low(nt_lo[:, j, :], bank[:, :], nt_hi[:, j, :], nt_high, 4 * f + (j + 1), nt_split)

            def turn_blocks(dst, src, j, ready, ready_at, turned):
                dve.wait_ge(ready, ready_at)
                nc.vector.transpose(dst.rearrange("p m (c j b) -> p j c m b", c=NT, j=NT)[:, j, :, :, :].bitcast(U32),
                                    src[:, j, :].rearrange("p (c m a) -> p c m a", c=NT, m=NT).bitcast(U32)
                                    ).then_inc(turned, 1)

            def turn_n(b, j):
                turn_blocks(n_blocks[:, :, 0:T], n, j, n_ready, 4 * b + (j + 1), n_turned)

            def turn_p(b, j):
                turn_blocks(p_blocks, prob, j, prob_ready, 4 * b + (j + 1), p_turned)

            def turn_n2(b, j):
                turn_blocks(n2_blocks, n2, j, n2_ready, 4 * b + (j + 1), n2_turned)

            def nt_rest_moved(b, c):
                low(rows(nt_lo[:, c, :]), chunk(n_t[:, :, 0:T], c), rows(nt_hi[:, c, :]), nt_high, 4 * b + (c + 5),
                    nt_split)

            def pt_rest_moved(b, c):
                low(rows(pt_lo[:, c, :]), chunk(p_t, c), rows(pt_hi[:, c, :]), pt_high, 4 * b + (c + 1), pt_split)

            def n2t_rest_moved(b, c):
                low(rows(n2t_lo[:, c, :]), chunk(n2_t, c), rows(n2t_hi[:, c, :]), n2t_high, 4 * b + (c + 1),
                    n2t_low_dve)

            def query_rest(b, j):
                low(q_lo[:, j, :], mm[QUERY_BANK[j]][:, :], q_hi[:, j, :], q_high, 4 * b + (j + 1), q_split,
                    bias=q_bias[:, j:j + 1])

            def value_rest(b, j):
                low(v_lo[:, j, :], mm[VALUE_BANK[j]][:, :], v_hi[:, j, :], v_high, 4 * b + (j + 1), v_split)

            def score_shift(b, j):
                at = 3 * (4 * b + j)
                dve.wait_ge(scores_ready, 4 * b + (j + 1))
                if j == 0:
                    dve.wait_ge(row_term_ready, 4 * b + 4)
                nc.vector.reduce_max(s_max[:, j:j + 1], mm[SCORE_BANK[j]][:, :], AX_X).then_inc(shift_step, 1)
                dve.wait_ge(shift_step, at + 1)
                nc.vector.tensor_tensor(out=s_top[:, j:j + 1], in0=s_max[:, j:j + 1], in1=row_term[:, j:j + 1],
                                        op=ALU.add).then_inc(shift_step, 1)
                dve.wait_ge(shift_step, at + 2)
                nc.vector.tensor_scalar(s_bias[:, j:j + 1], row_term[:, j:j + 1], s_top[:, j:j + 1], SCALE,
                                        ALU.subtract, ALU.mult).then_inc(shift_step, 1)

            def prob_rest(b, j):
                low(pt_lo[:, :, half(j)], fr[j % 2][:, :].rearrange("p (c k) -> p c k", c=NT),
                    pt_hi[:, :, half(j)], pt_high, 4 * b + (j + 1), pt_split)

            def add_attention(b, j):
                if j == 0:
                    nc.vector.reciprocal(p_rcp[:, :], p_sum[:, :]).then_inc(p_rcp_ready, 1)
                dve.wait_ge(h1_begun, 4 * b + (j + 1))
                if j == 0:
                    dve.wait_ge(p_rcp_ready, b + 1)
                dve.wait_ge(o_ready, 4 * b + (j + 1))
                nc.vector.scalar_tensor_tensor(out=h1[:, j, :], in0=mm[ATTEND_BANK[j]][:, :],
                                               scalar=p_rcp[:, j:j + 1], in1=h1[:, j, :], op0=ALU.mult,
                                               op1=ALU.add).then_inc(h1_ready, 1)

            def ln2_stats(b, j):
                at = LN2_STEPS * (4 * b + j)
                dve.wait_ge(h1_ready, 4 * b + (j + 1))
                nc.vector.bn_stats(stats2[:, j, :], h1[:, j, :]).then_inc(ln2_step, 1)
                dve.wait_ge(ln2_step, at + 1)
                nc.vector.memset(spare[:, :], 0.0)
                nc.vector.bn_aggr(mv2[:, j, :], stats2[:, j, :]).then_inc(ln2_step, 1)

            def ln2_scale(b, j):
                at = LN2_STEPS * (4 * b + j)
                dve.wait_ge(ln2_step, at + 2)
                refine([rstd2[:, k, j:j + 1] for k in range(4)], mv2[:, j, 1:2],
                       ln2_root, 2 * (4 * b + j) + 2, ln2_step, at + 2).then_inc(ln2_step, 1)
                dve.wait_ge(ln2_step, at + 5)
                nc.vector.scalar_tensor_tensor(out=rstd2[:, 4, j:j + 1], in0=mv2[:, j, 0:1], scalar=-1.0,
                                               in1=rstd2[:, 3, j:j + 1], op0=ALU.mult, op1=ALU.mult
                                               ).then_inc(n2_scale_ready, 1)

            def n2_rest(b, j):
                low(n2t_lo[:, :, half(j)], fr[j % 2][:, :].rearrange("p (c k) -> p c k", c=NT),
                    n2t_hi[:, :, half(j)], n2t_high, 4 * b + (j + 1), n2t_split)

            def add_ffn(b, j, h1_bias=h1_ffn, y=y):
                if j == 0 and y is not y_last:
                    dve.wait_ge(y_stored, 64 * b + 64)
                dve.wait_ge(h1_ffn_ready, 4 * b + (j + 1))
                dve.wait_ge(f_ready, 4 * b + (j + 1))
                nc.vector.scalar_tensor_tensor(out=y[:, j, :], in0=mm[FFN_BANK[j]][:, :], scalar=wscale[:, 0:1],
                                               in1=h1_bias[:, j, :], op0=ALU.mult, op1=ALU.add
                                               ).then_inc(y_ready, 1)

            dve.sem_inc(y_ready, NT)
            def merged_rest(dst, dst_hi, j, at):
                low(dst[:, j, :], mm[j][:, :], dst_hi[:, j, :], merged_hi, at + j + 1, merged_split)

            embed(0)
            channel_shift(0, 0)
            dve.wait_ge(consts_ready, 3)
            dve.wait_ge(tower_loaded, 80)
            dve.wait_ge(small_high, 2)
            nc.vector.scalar_tensor_tensor(out=conv_w_lo[:, :, :], in0=conv_w_sb[:, :, :], scalar=W_UP,
                                           in1=conv_w_hi[:, :, :], op0=ALU.mult, op1=ALU.subtract
                                           ).then_inc(small_split, 1)
            nc.vector.scalar_tensor_tensor(out=spos_lo[:, :, :], in0=spos_sb[:, :, :], scalar=W_UP,
                                           in1=spos_hi[:, :, :], op0=ALU.mult, op1=ALU.subtract
                                           ).then_inc(small_split, 1)
            channel_softmax(0, 0)
            x_rest(0)
            sel_rest(0, 0)
            for part in range(2):
                for c in range(NT):
                    col = (1 + part) * NT + c
                    nc.vector.tensor_scalar(b_wide[:, part, c, :], ones[:, :], b_qkv_sb[:, col:col + 1], None,
                                            ALU.mult).then_inc(wide_ready, 1)
            ln1_stats(X_BLK)
            dve.wait_ge(h_conv_ready, 1)
            ln1_stats(CONV_BLK)
            for j in range(NT):
                merged_rest(m_lo, m_hi, j, 0)
            channel_shift(0, 1)
            dve.wait_ge(h_ext_ready, 1)
            ln1_stats(XEXT_BLK)
            channel_softmax(0, 1)
            merged_rest(vo_lo, vo_hi, 0, NT)
            sel_rest(0, 1)
            dve.wait_ge(bias_mm_ready, 1)
            nc.vector.tensor_copy(q_bias[:, :], tp[0][:, 0:NT]).then_inc(bias_ready, 1)
            nc.vector.tensor_copy(bqbk[:, :], tp[0][:, NT:NT + 1]).then_inc(bias_ready, 1)
            dve.wait_ge(ffn_loaded, 32)
            nc.vector.tensor_reduce(wsum[:, :], w_ffn_sb[:, :, :].rearrange("p c t -> p (c t)"), AX_X, ALU.add,
                                    apply_absolute_value=True).then_inc(abs_ready, 1)
            merged_rest(vo_lo, vo_hi, 1, NT)
            dve.wait_ge(h_ext_ready, 2)
            ln1_stats(CEXT_BLK)
            ln1_finish_stats(0)
            ln1_scale(0)
            merged_rest(vo_lo, vo_hi, 2, NT)
            dve.wait_ge(bias_mm_ready, 2)
            nc.vector.tensor_copy(key_row[:, :], tp[1][:, :]).then_inc(bias_ready, 1)
            nt_rest(0, 0, fr[0])
            nt_rest(0, 1, fr[1])
            embed(1)
            channel_shift(1, 0)
            merged_rest(vo_lo, vo_hi, 3, NT)
            nt_rest(0, 2, fr[0])
            nt_rest(0, 3, fr[1])
            channel_softmax(1, 0)
            dve.wait_ge(bias_mm_ready, 3)
            dve.wait_ge(out_loaded, 48)
            nc.vector.tensor_tensor(out=attn_bias[:, :], in0=tp[0][:, :], in1=b_out_sb[:, :],
                                    op=ALU.add).then_inc(bias_ready, 1)
            dve.wait_ge(abs_total, 1)
            nc.vector.tensor_scalar(wscale[:, 0:1], tp[1][:, 0:1], 1.0 / (T * T), None, ALU.mult
                                    ).then_inc(tern_step, 1)
            dve.wait_ge(tern_step, 1)
            nc.vector.tensor_scalar(wscale[:, 1:2], wscale[:, 0:1], W_EPS, 0.5, ALU.add, ALU.mult
                                    ).then_inc(tern_step, 1)
            dve.wait_ge(tern_step, 2)
            nc.vector.tensor_scalar(wscale[:, 2:3], wscale[:, 1:2], -1.0, None, ALU.mult).then_inc(tern_step, 1)
            dve.wait_ge(tern_step, 3)
            nc.vector.tensor_scalar(below[:, :, :], w_ffn_sb[:, :, :], wscale[:, 2:3], None, ALU.is_lt
                                    ).then_inc(tern_step, 1)
            dve.wait_ge(bias_ready, 4)
            query_rest(0, 0)
            dve.wait_ge(tern_step, 4)
            nc.vector.scalar_tensor_tensor(out=tern[:, :, :], in0=w_ffn_sb[:, :, :], scalar=wscale[:, 1:2],
                                           in1=below[:, :, :], op0=ALU.is_gt, op1=ALU.subtract
                                           ).then_inc(tern_ready, 1)
            x_rest(1)
            query_rest(0, 1)
            sel_rest(1, 0)
            query_row_terms(0, range(NT))
            query_rest(0, 2)
            ln1_stats(X_BLK)
            query_rest(0, 3)
            dve.wait_ge(h_conv_ready, 2)
            ln1_stats(CONV_BLK)
            channel_shift(1, 1)
            channel_softmax(1, 1)
            dve.wait_ge(h_ext_ready, 3)
            ln1_stats(XEXT_BLK)
            value_rest(0, 0)
            sel_rest(1, 1)
            value_rest(0, 1)
            value_rest(0, 2)
            dve.wait_ge(h_ext_ready, 4)
            ln1_stats(CEXT_BLK)
            ln1_finish_stats(1)
            ln1_scale(1)
            value_rest(0, 3)
            embed(2)
            channel_shift(2, 0)

            def batch(b, prev, tower, front_next, embed_next):
                f, g, e = b + 1, b + 2, b + 3
                if not prev:
                    channel_softmax(g, 0)
                score_shift(b, 0)
                if tower and prev:
                    x_rest_moved(b)
                elif tower:
                    x_rest(g)
                turn_p(b, 0)
                score_shift(b, 1)
                if tower and prev:
                    sel_rest_moved(b)
                elif tower:
                    sel_rest(g, 0)
                turn_p(b, 1)
                score_shift(b, 2)
                if front_next and prev:
                    channel_softmax(e, 0)
                if prev:
                    for c in DVE_CHUNKS:
                        n2t_rest_moved(b - 1, c)
                score_shift(b, 3)
                turn_p(b, 2)
                turn_p(b, 3)
                if front_next and prev:
                    turn_front(e)
                if tower and prev:
                    ln1_stats(X_BLK)
                if prev:
                    for c in DVE_CHUNKS:
                        nt_rest_moved(b, c)
                else:
                    for c in range(NT):
                        nt_rest(f, c, (fr + tp)[c])
                if not prev:
                    embed(e)
                    channel_shift(e, 0)
                    channel_softmax(e, 0)
                    turn_front(e)
                if tower:
                    channel_shift(g, 1)
                if prev:
                    add_ffn(b - 1, 0)
                    add_ffn(b - 1, 1)
                if tower:
                    channel_softmax(g, 1)
                    dve.wait_ge(h_conv_ready, g + 1)
                    ln1_stats(CONV_BLK)
                if prev:
                    add_ffn(b - 1, 2)
                query_row_terms(f, (0,))
                if tower:
                    sel_rest(g, 1)
                if prev:
                    add_ffn(b - 1, 3)
                if tower:
                    dve.wait_ge(h_ext_ready, 2 * g + 1)
                    ln1_stats(XEXT_BLK)
                    if not prev:
                        ln1_stats(X_BLK)
                query_rest(f, 0)
                query_row_terms(f, (1, 2, 3))
                query_rest(f, 1)
                pt_rest_moved(b, 3)
                if tower:
                    dve.wait_ge(h_ext_ready, 2 * g + 2)
                    ln1_stats(CEXT_BLK)
                    ln1_finish_stats(g)
                if tower:
                    ln1_scale(g)
                query_rest(f, 2)
                if tower:
                    turn_n(g, 0)
                query_rest(f, 3)
                if tower:
                    turn_n(g, 1)
                add_attention(b, 0)
                ln2_stats(b, 0)
                if tower:
                    turn_n(g, 2)
                    turn_n(g, 3)
                for j in range(NT):
                    if j < NT - 1:
                        add_attention(b, j + 1)
                    ln2_scale(b, j)
                    if j < NT - 1:
                        ln2_stats(b, j + 1)
                    if j == NT - 1:
                        value_rest(f, 0)
                    turn_n2(b, j)
                value_rest(f, 1)
                value_rest(f, 2)
                if embed_next:
                    embed(e + 1)
                value_rest(f, 3)
                if embed_next:
                    channel_shift(e + 1, 0)

            batch(0, False, True, True, True)
            with dve.Fori(1, B - 4) as b:
                batch(b, True, True, True, True)
            batch(B - 4, True, True, True, False)
            batch(B - 3, True, True, False, False)
            batch(B - 2, True, False, False, False)

            last, before = B - 1, B - 2
            score_shift(last, 0)
            score_shift(last, 1)
            score_shift(last, 2)
            prob_rest(last, 0)
            score_shift(last, 3)
            prob_rest(last, 1)
            for c in DVE_CHUNKS:
                n2t_rest_moved(before, c)
            prob_rest(last, 2)
            prob_rest(last, 3)
            add_attention(last, 0)
            ln2_stats(last, 0)
            for j in range(NT):
                if j < NT - 1:
                    add_attention(last, j + 1)
                ln2_scale(last, j)
                if j < NT - 1:
                    ln2_stats(last, j + 1)
                if j > 0:
                    add_ffn(before, j - 1)
            n2_rest(last, 0)
            add_ffn(before, NT - 1)
            for j in range(1, NT):
                n2_rest(last, j)
                add_ffn(last, j - 1, h1_ffn_last, y_last)
            add_ffn(last, NT - 1, h1_ffn_last, y_last)


def position_table():
    import numpy as np
    depth = P // 2
    times = np.arange(T, dtype=np.float32)[:, None]
    depths = np.arange(depth, dtype=np.float32)[None, :] / np.float32(depth)
    rate = (np.float32(1.0) / np.power(np.float32(10000.0), depths)).astype(np.float32)
    angle = (times * rate).astype(np.float32)
    table = np.concatenate([np.sin(angle), np.cos(angle)], axis=-1).astype(np.float32)
    return np.ascontiguousarray(table.reshape(NT, P, P).transpose(1, 0, 2))


def kernel(x, L0_tok_emb_table, L0_tok_conv_w, L0_tok_conv_b, L0_tok_spos0, L0_tok_spos1, L0_attn_w_qkv,
           L0_attn_b_qkv, L0_attn_w_out, L0_attn_b_out, L0_ffn_weight, L0_ffn_bias):
    import numpy as np
    import concourse.bacc as bacc
    from concourse.bass_utils import run_bass_kernel_spmd

    B = x.shape[0]
    cols = [
        ("ids", np.asarray(x).reshape(B * NT, P).T),
        ("emb", L0_tok_emb_table),
        ("pos", position_table()),
        ("conv_w", np.asarray(L0_tok_conv_w).transpose(1, 2, 0)),
        ("conv_b", np.asarray(L0_tok_conv_b).reshape(P, 1)),
        ("spos0", L0_tok_spos0),
        ("spos1", L0_tok_spos1),
        ("w_qkv", L0_attn_w_qkv),
        ("b_qkv", np.asarray(L0_attn_b_qkv).reshape(3 * NT, P).T),
        ("w_out_t", np.asarray(L0_attn_w_out).T),
        ("b_out", L0_attn_b_out),
        ("w_ffn_t", np.asarray(L0_ffn_weight).T),
        ("b_ffn", L0_ffn_bias),
    ]
    nc = bacc.Bacc("TRN2", target_bir_lowering=False, num_devices=1)
    arrays, args = {}, []
    for name, a in cols:
        a = np.ascontiguousarray(a)
        arrays[f"in_{name}"] = a
        args.append(nc.dram_tensor(f"in_{name}", a.shape, mybir.dt.from_np(a.dtype), kind="ExternalInput").ap())
    args.append(nc.dram_tensor("out_h", (B, T, T), F32, kind="ExternalOutput").ap())
    lm_tower(nc, *args)
    r = run_bass_kernel_spmd(nc, [arrays], core_ids=[0])
    return r.results[0]["out_h"]
```
